# Optimizing a Trainium2 kernel written in Bass

```python
import numpy as np
import jax
import jax.numpy as jnp

def _softmax(x, axis=-1):
    return jax.nn.softmax(x, axis=axis)

def _gelu(x):
    return jax.nn.gelu(x, approximate=True)

def _silu(x):
    return jax.nn.silu(x)

def _sigmoid(x):
    return jax.nn.sigmoid(x)

def _layernorm(x, axis=-1, eps=1e-05):
    m = jnp.mean(x, axis=axis, keepdims=True)
    v = jnp.var(x, axis=axis, keepdims=True)
    return (x - m) / jnp.sqrt(v + eps)

def _scatter_add(tgt, idx, src, axis=0):
    return tgt.at[idx].add(src)

def _segment_sum(src, seg, n):
    return jax.ops.segment_sum(src, seg, n)
kernel_name = 'mk_seq_preln_d1_jaxref_r4_a699bd'

def setup_inputs(seed: int=0):
    np.random.seed(seed)
    _w = jnp.asarray

    def _L0_attn_setup():
        import jax, jax.numpy as jnp
        import numpy as np
        from jax import lax
        DIM = 256
        B, N = (4, 1024)

        def _rmsnorm(x, gamma):
            scale = jnp.asarray(x.shape[-1], x.dtype) ** 0.5
            norm = jnp.sqrt(jnp.sum(x * x, axis=-1, keepdims=True))
            return x / jnp.maximum(norm, 1e-12) * scale * gamma
        key = jax.random.key(seed)
        k1, k2 = jax.random.split(key)
        x = jax.random.normal(k1, (B, N, DIM), dtype=jnp.float32)
        w_qkva = jax.random.normal(k2, (3 * DIM, DIM), dtype=jnp.float32) * DIM ** (-0.5)
        gamma = jnp.ones((DIM,), dtype=jnp.float32)
        return {'x': x, 'w_qkva': w_qkva, 'gamma': gamma}
    _L0_attn_in = _L0_attn_setup()

    def _L0_ffn_setup():
        import jax, jax.numpy as jnp
        import numpy as np
        B, L, M = (4, 512, 256)
        G, E = (8, 8)
        CAP_FACTOR = 2.0

        def _ffn_size(m, widening=8.0):
            f = int(widening * m) * 2 // 3
            return f + (8 - f) % 8
        H = _ffn_size(M)

        def _gating_top2(logits, C):
            Gd, Sd, Ed = logits.shape
            raw = jax.nn.softmax(logits, axis=-1)
            idx1 = jnp.argmax(raw, axis=-1)
            m1 = jax.nn.one_hot(idx1, Ed, dtype=logits.dtype)
            gate1 = jnp.sum(raw * m1, axis=-1)
            rest = raw * (1.0 - m1)
            idx2 = jnp.argmax(rest, axis=-1)
            m2 = jax.nn.one_hot(idx2, Ed, dtype=logits.dtype)
            gate2 = jnp.sum(rest * m2, axis=-1)
            p1 = jnp.cumsum(m1, axis=-2) - m1
            m1 = m1 * (p1 < C).astype(m1.dtype)
            p1 = jnp.sum(p1 * m1, axis=-1)
            m1_flat = jnp.sum(m1, axis=-1)
            m1_count = jnp.sum(m1, axis=-2)
            p2 = jnp.cumsum(m2, axis=-2) - m2 + m1_count[:, None, :]
            m2 = m2 * (p2 < C).astype(m2.dtype)
            p2 = jnp.sum(p2 * m2, axis=-1)
            m2_flat = jnp.sum(m2, axis=-1)
            gate1 = gate1 * m1_flat
            gate2 = gate2 * m2_flat
            c1 = (gate1[..., None] * jax.nn.one_hot(idx1, Ed, dtype=jnp.float32))[..., None] * jax.nn.one_hot(p1.astype(jnp.int32), C, dtype=jnp.float32)[:, :, None, :]
            c2 = (gate2[..., None] * jax.nn.one_hot(idx2, Ed, dtype=jnp.float32))[..., None] * jax.nn.one_hot(p2.astype(jnp.int32), C, dtype=jnp.float32)[:, :, None, :]
            combine = (c1 + c2).astype(logits.dtype)
            dispatch = (combine != 0).astype(logits.dtype)
            return (dispatch, combine)
        key = jax.random.key(seed)
        k0, k1, k2, k3, k4 = jax.random.split(key, 5)
        return {'inputs': jax.random.normal(k0, (B, L, M), jnp.float32), 'router_w': jax.random.normal(k1, (M, E), jnp.float32) * 0.02, 'w0_kernel': jax.random.normal(k2, (E, M, H), jnp.float32) * 0.02, 'w1_kernel': jax.random.normal(k3, (E, M, H), jnp.float32) * 0.02, 'wo_kernel': jax.random.normal(k4, (E, H, M), jnp.float32) * 0.02}
    _L0_ffn_in = _L0_ffn_setup()
    _d = {'L0_attn_x': _L0_attn_in['x'], 'L0_attn_w_qkva': _L0_attn_in['w_qkva'], 'L0_attn_gamma': _L0_attn_in['gamma'], 'L0_ffn_router_w': _L0_ffn_in['router_w'], 'L0_ffn_w0_kernel': _L0_ffn_in['w0_kernel'], 'L0_ffn_w1_kernel': _L0_ffn_in['w1_kernel'], 'L0_ffn_wo_kernel': _L0_ffn_in['wo_kernel']}
    _x0 = _d['L0_attn_x']
    _d['L0_attn_x'] = jax.random.normal(jax.random.fold_in(jax.random.key(seed), 1), (8, 1024, 256), dtype=_x0.dtype)
    del _x0
    return _d

def reference(L0_attn_x, L0_attn_w_qkva, L0_attn_gamma, L0_ffn_router_w, L0_ffn_w0_kernel, L0_ffn_w1_kernel, L0_ffn_wo_kernel):

    def _L0_attn_ref(x, w_qkva, gamma):
        import jax, jax.numpy as jnp
        import numpy as np
        from jax import lax
        DIM = 256
        B, N = (4, 1024)

        def _rmsnorm(x, gamma):
            scale = jnp.asarray(x.shape[-1], x.dtype) ** 0.5
            norm = jnp.sqrt(jnp.sum(x * x, axis=-1, keepdims=True))
            return x / jnp.maximum(norm, 1e-12) * scale * gamma
        h = _rmsnorm(x, gamma)
        qkva = jnp.einsum('bnd,ed->bne', h, w_qkva)
        q, kv, a = jnp.split(qkva, 3, axis=-1)
        a = jax.nn.sigmoid(a)

        def binary_operator(e_i, e_j):
            a_i, kv_i = e_i
            a_j, kv_j = e_j
            return (a_j * a_i, a_j * kv_i + kv_j)
        _, y = lax.associative_scan(binary_operator, (a, kv), axis=1)
        return q * y

    def _L0_ffn_ref(inputs, router_w, w0_kernel, w1_kernel, wo_kernel):
        import jax, jax.numpy as jnp
        import numpy as np
        B, L, M = (4, 512, 256)
        G, E = (8, 8)
        CAP_FACTOR = 2.0

        def _ffn_size(m, widening=8.0):
            f = int(widening * m) * 2 // 3
            return f + (8 - f) % 8
        H = _ffn_size(M)

        def _gating_top2(logits, C):
            Gd, Sd, Ed = logits.shape
            raw = jax.nn.softmax(logits, axis=-1)
            idx1 = jnp.argmax(raw, axis=-1)
            m1 = jax.nn.one_hot(idx1, Ed, dtype=logits.dtype)
            gate1 = jnp.sum(raw * m1, axis=-1)
            rest = raw * (1.0 - m1)
            idx2 = jnp.argmax(rest, axis=-1)
            m2 = jax.nn.one_hot(idx2, Ed, dtype=logits.dtype)
            gate2 = jnp.sum(rest * m2, axis=-1)
            p1 = jnp.cumsum(m1, axis=-2) - m1
            m1 = m1 * (p1 < C).astype(m1.dtype)
            p1 = jnp.sum(p1 * m1, axis=-1)
            m1_flat = jnp.sum(m1, axis=-1)
            m1_count = jnp.sum(m1, axis=-2)
            p2 = jnp.cumsum(m2, axis=-2) - m2 + m1_count[:, None, :]
            m2 = m2 * (p2 < C).astype(m2.dtype)
            p2 = jnp.sum(p2 * m2, axis=-1)
            m2_flat = jnp.sum(m2, axis=-1)
            gate1 = gate1 * m1_flat
            gate2 = gate2 * m2_flat
            c1 = (gate1[..., None] * jax.nn.one_hot(idx1, Ed, dtype=jnp.float32))[..., None] * jax.nn.one_hot(p1.astype(jnp.int32), C, dtype=jnp.float32)[:, :, None, :]
            c2 = (gate2[..., None] * jax.nn.one_hot(idx2, Ed, dtype=jnp.float32))[..., None] * jax.nn.one_hot(p2.astype(jnp.int32), C, dtype=jnp.float32)[:, :, None, :]
            combine = (c1 + c2).astype(logits.dtype)
            dispatch = (combine != 0).astype(logits.dtype)
            return (dispatch, combine)
        Bb, Ll, Mm = inputs.shape
        S = Bb * Ll // G
        x = inputs.reshape(G, S, Mm)
        logits = jnp.einsum('GSM,ME->GSE', x, router_w)
        cap = int(CAP_FACTOR * S / E)
        C = (cap + 3) // 4 * 4
        dispatch, combine = _gating_top2(logits, C)
        expert_inputs = jnp.einsum('GSEC,GSM->EGCM', dispatch, x)
        layer_w0 = jnp.einsum('EGCM,EMH->EGCH', expert_inputs, w0_kernel)
        layer_w1 = jnp.einsum('EGCM,EMH->EGCH', expert_inputs, w1_kernel)
        hidden = jax.nn.gelu(layer_w0, approximate=True) * layer_w1
        expert_outputs = jnp.einsum('EGCH,EHM->EGCM', hidden, wo_kernel)
        out = jnp.einsum('EGCM,GSEC->GSM', expert_outputs, combine)
        return out.reshape(Bb, Ll, Mm)
    x = L0_attn_x
    x = x + _L0_attn_ref(_layernorm(x, axis=-1), L0_attn_w_qkva, L0_attn_gamma)
    x = x + _L0_ffn_ref(_layernorm(x, axis=-1), L0_ffn_router_w, L0_ffn_w0_kernel, L0_ffn_w1_kernel, L0_ffn_wo_kernel)
    return x

_drawn_inputs = setup_inputs


def setup_inputs(seed=0):
    import zlib

    import numpy as np

    out = dict(_drawn_inputs(seed))
    spreads = {'L0_attn_gamma': (1.0, 0.2)}
    factors = {'L0_ffn_router_w': 8.0,
     'L0_ffn_w0_kernel': 8.0,
     'L0_ffn_w1_kernel': 8.0,
     'L0_ffn_wo_kernel': 8.0}
    for name, (base, spread) in spreads.items():
        noise = np.random.default_rng([zlib.crc32(name.encode()), seed]).standard_normal(out[name].shape)
        drawn = base * np.exp(spread * noise) if base else spread * noise
        out[name] = jnp.asarray(drawn.astype(out[name].dtype))
    for name, factor in factors.items():
        out[name] = (out[name] * factor).astype(out[name].dtype)
    return out
```

```python
from contextlib import ExitStack

import numpy as np

import concourse.bass as bass
from concourse import mybir

F32 = mybir.dt.float32
F32R = mybir.dt.float32r
BF16 = mybir.dt.bfloat16
I32 = mybir.dt.int32
ALU = mybir.AluOpType
ACT = mybir.ActivationFunctionType
AXX = mybir.AxisListType.X
P = 128
PREPARE = 6
LN_EPS = 1e-5
NORM_MIN = 1e-12


FREE_SCATTER = 1
FREE_MUL = 2
FREE_DOWN = 3
FREE_ROWS = 2


class Turn:

    def __init__(self, value, least=None):
        self.value = value
        self.fixed = least is None
        self.least = value if least is None else least

    def plus(self, n):
        return Turn(self.value + n, None if self.fixed else self.least + n)

    def count(self, per, more):
        return self.value * per + more


def wait(eng, sem, turn, per, more):
    least = turn.least * per + more
    if turn.fixed and least <= 0:
        return
    assert least > 0
    eng.wait_ge(sem, turn.count(per, more))


class Chain:

    def __init__(self, eng, sem, per):
        self.eng, self.sem, self.per = eng, sem, per

    def begin(self, turn, done=0):
        self.turn, self.n = turn, done

    def link(self, instruction):
        self.n += 1
        instruction.then_inc(self.sem, 1)
        wait(self.eng, self.sem, self.turn, self.per, self.n)

    def end(self):
        assert self.n == self.per, (self.n, self.per)


def build(nc, x_in, w_qkva, gamma_in, router_in, w0_in, w1_in, wo_in, out):
    G, S, D = x_in.shape
    E, _, H = w0_in.shape
    CAP = (2 * S // E + 3) // 4 * 4
    KD = D // P
    TILES = S // P
    HT = TILES // 2
    T = HT * P
    NCH = 3 * D // P
    HC = -(-H // P)
    HLAST = H - (HC - 1) * P
    ROW = D + 4
    GT1, GT2, EX1, TOK = D, D + 1, D + 2, D + 3
    ESLOTS = G * CAP
    NSLOT = E * ESLOTS
    FT = ESLOTS // T
    FJ = T // P
    NTOK = G * S
    WCOL = 2 * KD * P + D
    STAGES = 4
    XSLOTS = 3
    XG = TILES * D
    assert (G, KD, TILES, FT, T, FJ) == (8, 2, 8, 4, 512, 4) and E * 16 <= P

    slots = nc.dram_tensor("slots", [NSLOT + 2 * S, ROW], F32, kind="Internal").ap()
    sums = nc.dram_tensor("sums", [NTOK + T, D], F32, kind="Internal").ap()

    with ExitStack() as ctx:
        def sb(name, shape, dt=F32):
            return ctx.enter_context(nc.sbuf_tensor(name, shape, dt))

        def sem(name):
            return ctx.enter_context(nc.semaphore(name))

        ROWS2 = 2 * FJ * ROW
        xring = sb("xring", [P, 2 * XG + ROWS2])
        assert ROWS2 >= XG
        rows = sb("rows", [P, TILES, ROW])
        xn = sb("xn", [P, HT, D])
        x2n = sb("x2n", [P, 2, HT, D])
        xThi = sb("xThi", [P, 2, KD, T], F32R)
        xTlo = sb("xTlo", [P, 2, KD, T], F32R)
        wThi = sb("wThi", [P, KD, 3 * D], F32R)
        wTlo = sb("wTlo", [P, KD, 3 * D], F32R)
        sig = sb("sig", [P, KD, T])
        y = sb("y", [P, 2, KD, T])
        z = sb("z", [P, 2, KD, T])
        x2nT = sb("x2nT", [P, KD, T])
        fill = sb("fill", [P, FJ, ROW])
        whi = sb("whi", [P, HC, WCOL], F32R)
        wlo = sb("wlo", [P, HC, WCOL], F32R)
        stage = sb("stage", [P, STAGES, WCOL])
        hhi = sb("hhi", [P, 3, T], F32R)
        hlo = sb("hlo", [P, 3, T], F32R)
        ident = sb("ident", [P, P])
        before = sb("before", [P, P], BF16)
        ones = sb("ones", [P, P], BF16)
        router = sb("router", [P, KD, E])
        gamma = sb("gamma", [P, KD])
        nhalf = sb("nhalf", [P, HT])
        phalf = sb("phalf", [P, HT])
        rank = sb("rank", [P, E])
        dump = sb("dump", [P, 2 * TILES])
        slotbase = sb("slotbase", [P, 1])
        tokid = sb("tokid", [P, TILES])
        expert_no = sb("expert_no", [P, 1])
        st1 = sb("st1", [P, 2, HT, 6])
        mv1 = sb("mv1", [P, 2, HT, 2])
        ve1 = sb("ve1", [P, 2, 2, HT])
        pw1 = sb("pw1", [P, 2, 2, HT])
        nrm = sb("nrm", [P, HT])
        rec = sb("rec", [P, HT])
        sc1 = sb("sc1", [P, 2, HT])
        nb1 = sb("nb1", [P, 2, HT])
        st2 = sb("st2", [P, 2, HT, 6])
        mv2 = sb("mv2", [P, 2, HT, 2])
        ve2 = sb("ve2", [P, 2, HT])
        sc2 = sb("sc2", [P, 2, HT])
        nb2 = sb("nb2", [P, 2, HT])
        mx = sb("mx", [P, TILES])
        dl = sb("dl", [P, TILES, E])
        ex = sb("ex", [P, TILES, E])
        sm = sb("sm", [P, TILES])
        rs = sb("rs", [P, TILES])
        raw = sb("raw", [P, TILES, E])
        eq = sb("eq", [P, TILES, E])
        gate = sb("gate", [P, 2, TILES])
        top = sb("top", [P, 2, TILES])
        mask = sb("mask", [P, 2, TILES, E], BF16)
        cnt1 = sb("cnt1", [P, E])
        pos = sb("pos", [P, 2, TILES, E])
        psel = sb("psel", [P, 2, TILES])
        keep = sb("keep", [P, 2, TILES])
        slotf = sb("slotf", [P, 2, TILES])
        sloti = sb("sloti", [P, 2, TILES], I32)
        gsel = sb("gsel", [P, 2, FJ])
        gslot = sb("gslot", [P, 2, FJ])

        wraw = x2n[:, :, :, :].rearrange("p a b c -> p (a b c)")[:, 0:NCH * D].rearrange("p (c d) -> p c d", c=NCH)
        rows2 = xring[:, 2 * XG:2 * XG + ROWS2].rearrange("p (b j c) -> p b j c", b=2, j=FJ)
        ysb = xring[:, 0:2 * FJ * D].rearrange("p (b j c) -> p b j c", b=2, j=FJ)
        gel = sig
        hf = y[:, 0]

        bank = [ctx.enter_context(nc.psum_tensor(f"bank{i}", [P, 512], F32)) for i in range(8)]
        tA = bank[0:2]
        pa, pkv, pq = bank[2], bank[3], bank[4]
        tC = bank[5:7]
        lg = bank[7][:, 0:TILES * E]
        cum = bank[7][:, 128:128 + 2 * TILES * E]
        tot = bank[7][:, 384:384 + E]
        up = [bank[2:4], bank[5:7]]
        yb = [bank[4], bank[7]]

        x_loaded = [sem(f"x_loaded{h}") for h in range(2)]
        consts_loaded = sem("consts_loaded")
        wq_loaded = sem("wq_loaded")
        consts_made = sem("consts_made")
        fill_made = sem("fill_made")
        fill_id = sem("fill_id")
        prefilled = sem("prefilled")
        sums_tail = sem("sums_tail")
        wq_t = sem("wq_t")
        wq_hi = sem("wq_hi")
        wq_lo = sem("wq_lo")
        consts_raw = sem("consts_raw")
        stats_chain1 = sem("stats_chain1")
        fac_chain1 = sem("fac_chain1")
        stats_chain2 = sem("stats_chain2")
        choose_chain = sem("choose_chain")
        place_chain = sem("place_chain")
        gate_chain = sem("gate_chain")
        stats1 = sem("stats1")
        pow1 = sem("pow1")
        fac1 = sem("fac1")
        norm1 = sem("norm1")
        t1 = sem("t1")
        split_hi = sem("split_hi")
        split_lo = sem("split_lo")
        a_done = sem("a_done")
        kv_done = sem("kv_done")
        q_done = sem("q_done")
        sig_done = sem("sig_done")
        scan_done = sem("scan_done")
        z_done = sem("z_done")
        back = sem("back")
        x1_done = sem("x1_done")
        stats2 = sem("stats2")
        pow2 = sem("pow2")
        fac2 = sem("fac2")
        norm2 = sem("norm2")
        rows_x = sem("rows_x")
        x1_stored = [sem(f"x1_stored{h}") for h in range(2)]
        t2 = sem("t2")
        x2nT_done = sem("x2nT_done")
        logits = sem("logits")
        shifted = sem("shifted")
        exps = sem("exps")
        masks = sem("masks")
        counted = sem("counted")
        routed = sem("routed")
        scattered = sem("scattered")
        scatter_done = sem("scatter_done")
        w_staged = [sem(f"w_staged{i}") for i in range(STAGES)]
        w_hi0 = sem("w_hi0")
        w_split0 = sem("w_split0")
        w_hi = sem("w_hi")
        w_split = sem("w_split")
        rows_loaded = [sem(f"rows_loaded{i}") for i in range(2)]
        ft = sem("ft")
        fx_hi = sem("fx_hi")
        fx_lo = sem("fx_lo")
        gate_done = sem("gate_done")
        up0 = sem("up0")
        up1 = sem("up1")
        gelu_done = sem("gelu_done")
        mul_done = sem("mul_done")
        h_hi = sem("h_hi")
        h_lo = sem("h_lo")
        down = sem("down")
        y_read = sem("y_read")
        added = sem("added")
        rows_free = sem("rows_free")
        apart = {eng: sem(f"apart{i}") for i, eng in enumerate((nc.sync, nc.vector, nc.gpsimd))}
        out_stored = sem("out_stored")

        block = ctx.enter_context(nc.Block())

        def stand_apart(eng):
            eng.sem_inc(apart[eng], 1)

        def xslot(g, h, j, n=1):
            at = (g.value % XSLOTS) * XG + (h * HT + j) * D
            return xring[:, bass.ds(at, n * D)]

        def pipeline(eng, stage_fn):
            for i in range(-1, 2):
                stage_fn(Turn(i))
            with eng.Fori(2, G - 1) as i:
                stage_fn(Turn(i, 2))
            for i in range(G - 1, G + 2):
                stage_fn(Turn(i))

        def live(i, ahead):
            return True if not i.fixed else 0 <= i.value + ahead < G

        def experts(eng, fn):
            with eng.Fori(0, E - 1) as e:
                fn(Turn(e, 0), False)
            fn(Turn(E - 1), True)

        def weight_loads(sync, e, hc):
            n = P if hc < HC - 1 else HLAST
            c = slice(hc * P, hc * P + n)
            s = hc % STAGES
            ev = e.value
            for k, w in enumerate((w0_in, w1_in)):
                src = w[bass.ds(ev, 1), :, c].rearrange("o (k p) h -> p (o k) h", p=P)
                dst = stage[:, s, k * KD * P:(k + 1) * KD * P].rearrange("p (k h) -> p k h", k=KD)[:, :, 0:n]
                sync.dma_start(dst, src).then_inc(w_staged[s], 16)
            sync.dma_start(stage[0:n, s, 2 * KD * P:WCOL],
                           wo_in[bass.ds(ev, 1), c, :].rearrange("o h m -> h (o m)")).then_inc(w_staged[s], 16)

        per_stage = [len(range(s, HC, STAGES)) for s in range(STAGES)]

        def staged(eng, e, hc):
            s = hc % STAGES
            wait(eng, w_staged[s], e, 48 * per_stage[s], 48 * (hc // STAGES + 1))

        def chunk_before(hc):
            return hc - STAGES if hc >= STAGES else max(c for c in range(HC) if c % STAGES == hc) - HC

        @block.sync
        def _(sync):
            def wait_apart(signal, turn, per, more):
                wait(sync, signal, turn, per, more)
                if not turn.fixed:
                    stand_apart(sync)

            def ring_half(g, h):
                at = (g.value % XSLOTS) * XG + h * HT * D
                return xring[:, bass.ds(at, HT * D)].rearrange("p (j c) -> p j c", j=HT)

            def load_x(g, h):
                if not g.fixed or g.value >= XSLOTS:
                    wait_apart(x1_stored[h], g, 16, -16 * (XSLOTS - 1))
                    wait_apart(norm2, g, 2, -2 * XSLOTS + h + 1)
                wait_apart(x_loaded[h], g, 16, 0)
                sync.dma_start(
                    ring_half(g, h),
                    x_in[bass.ds(g.value, 1), h * T:(h + 1) * T, :].rearrange("o (j p) c -> p (o j) c", p=P),
                ).then_inc(x_loaded[h], 16)

            def store_x1(g, h):
                wait_apart(x1_done, g, 2, h + 1)
                wait_apart(x1_stored[h], g, 16, 0)
                sync.dma_start(
                    sums[0:NTOK, :].rearrange("(g t) c -> g t c", g=G)[bass.ds(g.value, 1), h * T:(h + 1) * T, :]
                    .rearrange("o (j p) c -> p (o j) c", p=P),
                    ring_half(g, h),
                ).then_inc(x1_stored[h], 16)

            load_x(Turn(0), 0)
            sync.dma_start(wraw, w_qkva.rearrange("(c p) d -> p c d", p=P)).then_inc(wq_loaded, 16)
            sync.dma_start(gamma[:, :], gamma_in.rearrange("(k p) -> p k", p=P),
                           allow_slow_non_contiguous=True).then_inc(consts_loaded, 16)
            sync.dma_start(router[:, :, :], router_in.rearrange("(k p) e -> p k e", p=P)).then_inc(consts_loaded, 16)
            load_x(Turn(0), 1)
            load_x(Turn(1), 0)
            load_x(Turn(1), 1)
            for hc in range(STAGES):
                weight_loads(sync, Turn(0), hc)
            sync.wait_ge(fill_made, 1)
            sync.dma_start(sums[NTOK:NTOK + T, :].rearrange("(p j) c -> p j c", p=P),
                           fill[:, :, 0:D]).then_inc(sums_tail, 16)
            for n in range(E * FT):
                sync.dma_start(slots[n * T:(n + 1) * T, :].rearrange("(p j) c -> p j c", p=P),
                               fill[:, :, :]).then_inc(prefilled, 16)
                if n == FT:
                    load_x(Turn(2), 0)
                    load_x(Turn(2), 1)

            def step(i):
                for h in range(2):
                    if not i.fixed or i.value < G + 1:
                        store_x1(i.plus(-1), h)
                    if not i.fixed or i.value + 2 < G:
                        load_x(i.plus(2), h)

            step(Turn(1))
            for hc in range(STAGES, HC):
                sync.wait_ge(w_split0, chunk_before(hc) + 1)
                weight_loads(sync, Turn(0), hc)
            with sync.Fori(2, G - 2) as i:
                step(Turn(i, 2))
            for i in range(G - 2, G + 1):
                step(Turn(i))

            def load_rows(e, t):
                wait_apart(rows_free, e, FT, t + 1)
                sync.wait_ge(scatter_done, 2 * (t + 1) + FREE_SCATTER)
                src = slots[0:NSLOT, :].rearrange("(e s) c -> e s c", e=E)[bass.ds(e.value, 1), t * T:(t + 1) * T, :]
                sync.dma_start(rows2[:, t % 2], src.rearrange("o (p j) c -> p (o j) c", p=P)).then_inc(
                    rows_loaded[t % 2], 16)

            last_there = G - 1 - (G - 1 - 2) % XSLOTS
            for h in range(2):
                sync.wait_ge(x1_stored[h], 16 * (last_there + 1))
            sync.wait_ge(norm2, 2 * (last_there + 1))
            load_rows(Turn(0), 0)
            sync.wait_ge(w_split0, HC)

            def expert(e, last):
                for t in range(FT):
                    if t < FT - 1:
                        load_rows(e, t + 1)
                    elif not last:
                        load_rows(e.plus(1), 0)
                        for hc in range(HC):
                            wait_apart(w_split, e, HC, HC + chunk_before(hc) + 1)
                            weight_loads(sync, e.plus(1), hc)
                    if last:
                        wait_apart(rows_free, e, FT, t + 1 + FREE_ROWS)
                        a, b = t * NTOK // FT, (t + 1) * NTOK // FT
                        sync.dma_start(out.rearrange("g s c -> (g s) c")[a:b, :].rearrange("(p j) c -> p (j c)", p=P),
                                       sums[a:b, :].rearrange("(p j) c -> p (j c)", p=P)).then_inc(out_stored, 16)

            experts(sync, expert)
            sync.wait_ge(out_stored, 16 * FT)

        @block.gpsimd
        def _(pool):
            pool.sem_inc(scatter_done, FREE_SCATTER)
            pool.sem_inc(rows_free, FREE_ROWS)
            pool.memset(ident[:, :], 0.0).then_inc(consts_raw, 1)
            pool.memset(before[:, :], 1.0).then_inc(consts_raw, 1)
            pool.wait_ge(consts_raw, 2)
            pool.affine_select(out=ident[:, :], in_=ident[:, :], compare_op=ALU.not_equal, fill=1.0, base=0,
                               pattern=[[-1, P]], channel_multiplier=1)
            pool.affine_select(out=before[:, :], in_=before[:, :], compare_op=ALU.is_gt, fill=0.0, base=0,
                               pattern=[[1, P]], channel_multiplier=-1)
            pool.memset(nhalf[:, :], -0.5)
            pool.memset(phalf[:, :], 0.5)
            pool.memset(ones[:, :], 1.0)
            pool.memset(fill[:, :, 0:TOK], 0.0)
            pool.iota(fill[:, :, TOK].bitcast(I32), pattern=[[1, FJ]], base=NTOK,
                      channel_multiplier=FJ).then_inc(fill_made, 1)
            pool.iota(rank[:, :], pattern=[[-1, E]], base=E, channel_multiplier=0,
                      allow_small_or_imprecise_dtypes=True)
            pool.iota(dump[:, :], pattern=[[P, 2 * TILES]], base=NSLOT, channel_multiplier=1,
                      allow_small_or_imprecise_dtypes=True)
            pool.iota(tokid[:, :], pattern=[[P, TILES]], base=0, channel_multiplier=1,
                      allow_small_or_imprecise_dtypes=True)
            pool.memset(slotbase[:, :], float(E * ESLOTS))
            pool.memset(expert_no[:, :], 0.0).then_inc(consts_made, 1)

            def first_weights(a, b):
                for hc in range(a, b):
                    staged(pool, Turn(0), hc)
                    pool.tensor_copy(whi[:, hc, :], stage[:, hc % STAGES, :]).then_inc(w_hi0, 1)
                    pool.wait_ge(w_hi0, hc + 1)
                    pool.tensor_tensor(wlo[:, hc, :], stage[:, hc % STAGES, :], whi[:, hc, :].bitcast(F32),
                                       ALU.subtract).then_inc(w_split0, 1)

            def powers1(g, h):
                wait(pool, stats1, g, 2, h + 1)
                pool.tensor_tensor(pw1[:, h, 0, :], ve1[:, h, 0, :], nhalf[:, :], ALU.pow)
                pool.tensor_tensor(pw1[:, h, 1, :], ve1[:, h, 1, :], phalf[:, :], ALU.pow).then_inc(pow1, 1)

            def powers2(g, h):
                wait(pool, stats2, g, 2, h + 1)
                pool.tensor_tensor(sc2[:, h, :], ve2[:, h, :], nhalf[:, :], ALU.pow).then_inc(pow2, 1)

            def scatter(g, k, a, b):
                if k == 0 and a == 0:
                    pool.wait_ge(prefilled, 16 * E * FT)
                    wait(pool, routed, g, 1, 1)
                    wait(pool, rows_x, g, 1, 1)
                for t in range(a, b):
                    pool.indirect_dma_start(slots[:, :], bass.IndirectOffsetOnAxis(sloti[:, k, t:t + 1], 0),
                                            rows[:, t, :], None).then_inc(scattered, 16)
                if k == 1 and b == TILES:
                    wait(pool, scattered, g, 16 * 2 * TILES, 16 * 2 * TILES)
                    pool.sem_inc(scatter_done, 1)

            def step(i):
                A, C, Dg = live(i, 1), live(i, -1), live(i, -2)
                if A:
                    powers1(i.plus(1), 0)
                if C:
                    powers2(i.plus(-1), 0)
                if Dg:
                    scatter(i.plus(-2), 0, 0, TILES // 2)
                if C:
                    powers2(i.plus(-1), 1)
                if Dg:
                    scatter(i.plus(-2), 0, TILES // 2, TILES)
                if A:
                    powers1(i.plus(1), 1)
                if Dg:
                    scatter(i.plus(-2), 1, 0, TILES)
                if i.fixed and i.value in (0, 1):
                    first_weights(*((0, STAGES) if i.value == 0 else (STAGES, HC)))

            pipeline(pool, step)

            pool.wait_ge(sums_tail, 16)
            for h in range(2):
                pool.wait_ge(x1_stored[h], 16 * G)

            def expert(e, last):
                for t in range(FT):
                    wait(pool, y_read, e, FT * FJ, FJ * (t + 1) + FJ)
                    stand_apart(pool)
                    for j in range(FJ):
                        idx = rows2[:, t % 2, j, TOK:TOK + 1].bitcast(I32)
                        pool.indirect_dma_start(sums[:, :], bass.IndirectOffsetOnAxis(idx, 0),
                                                ysb[:, t % 2, j, :], None, compute_op=ALU.add).then_inc(added, 16)
                    wait(pool, added, e, 16 * FJ * FT, 16 * FJ * (t + 1))
                    pool.sem_inc(rows_free, 1)

            experts(pool, expert)

        @block.scalar
        def _(act):
            act.sem_inc(y_read, FJ)
            act.wait_ge(consts_loaded, 32)

            def sigmoid(g, h, ch):
                wait(act, a_done, g, 4, 2 * h + ch + 1)
                act.activation(sig[:, ch, :], pa[:, :], ACT.Sigmoid).then_inc(sig_done, 1)

            def normalise1(g, h):
                wait(act, fac1, g, 2, h + 1)
                wait(act, t1, g, 2, h)
                for j in range(HT):
                    last = act.activation(xn[:, j, :], xslot(g, h, j), ACT.Identity,
                                          bias=nb1[:, h, j:j + 1], scale=sc1[:, h, j:j + 1])
                last.then_inc(norm1, 1)

            def split1(g, h):
                wait(act, t1, g, 2, h + 1)
                for k in range(KD):
                    act.activation(xThi[:, h, k, :], tA[k][:, :], ACT.Copy, scale=gamma[:, k:k + 1]).then_inc(split_hi, 1)

            def normalise2(g, h):
                wait(act, fac2, g, 2, h + 1)
                wait(act, t2, g, 2, h - 1)
                wait(act, rows_x, g, 1, 0)
                for j in range(HT):
                    last = act.activation(x2n[:, h, j, :], xslot(g, h, j), ACT.Identity,
                                          bias=nb2[:, h, j:j + 1], scale=sc2[:, h, j:j + 1])
                last.then_inc(norm2, 1)

            def copy_rows(g):
                wait(act, scatter_done, g, 1, FREE_SCATTER)
                wait(act, norm2, g, 2, 2)
                act.activation(rows[:, :, 0:D], x2n[:, :, :, :].rearrange("p h j c -> p (h j) c"),
                               ACT.Copy).then_inc(rows_x, 1)

            def read_t2(g, h):
                wait(act, t2, g, 2, h + 1)
                wait(act, logits, g, 2, h)
                for k in range(KD):
                    act.activation(x2nT[:, k, :], tC[k][:, :], ACT.Copy).then_inc(x2nT_done, 1)

            def exponent(g):
                wait(act, shifted, g, 1, 1)
                act.activation(ex[:, :, :], dl[:, :, :], ACT.Exp).then_inc(exps, 1)

            act.wait_ge(wq_t, 1)
            for k in range(KD):
                for a, b in ((0, 512), (512, NCH * P)):
                    act.activation(wThi[:, k, a:b], bank[2 * k + a // 512][:, 0:b - a], ACT.Copy).then_inc(wq_hi, 1)

            def step(i):
                A, B, C, Dg = live(i, 1), live(i, 0), live(i, -1), live(i, -2)
                if Dg:
                    copy_rows(i.plus(-2))
                if B:
                    sigmoid(i, 0, 0)
                if A:
                    normalise1(i.plus(1), 0)
                if B:
                    sigmoid(i, 0, 1)
                if C:
                    normalise2(i.plus(-1), 0)
                if A:
                    split1(i.plus(1), 0)
                if B:
                    sigmoid(i, 1, 0)
                if C:
                    normalise2(i.plus(-1), 1)
                    read_t2(i.plus(-1), 0)
                if A:
                    normalise1(i.plus(1), 1)
                if B:
                    sigmoid(i, 1, 1)
                if A:
                    split1(i.plus(1), 1)
                if C:
                    read_t2(i.plus(-1), 1)
                    exponent(i.plus(-1))

            pipeline(act, step)

            def prepare(e, t):
                for k in range(KD):
                    wait(act, ft, e, KD * FT, KD * t + k + 1)
                    act.activation(xThi[:, t % 2, k, :], tA[k][:, :], ACT.Copy).then_inc(fx_hi, 1)

            prepare(Turn(0), 0)
            for h in range(2):
                act.wait_ge(x1_stored[h], 16 * G)

            def next_weights(e, hc):
                staged(act, e.plus(1), hc)
                wait(act, down, e, HC * FT, HC * (FT - 1) + hc + 1 + FREE_DOWN)
                act.activation(whi[:, hc, :], stage[:, hc % STAGES, :], ACT.Copy).then_inc(w_hi, 1)

            def expert(e, last):
                for t in range(FT):
                    fetch = t == FT - 1 and not last
                    for hc in range(HC):
                        n = P if hc < HC - 1 else HLAST
                        c = HC * t + hc
                        wait(act, up0, e, HC * FT, c + 1)
                        act.activation(gel[0:n, hc % 2, :], up[hc % 2][0][0:n, :],
                                       ACT.Gelu_apprx_tanh).then_inc(gelu_done, 1)
                        wait(act, mul_done, e, HC * FT, c + 1 + FREE_MUL)
                        user = c - 3 if hc >= 3 else c - hc - HC + max(q for q in range(HC) if q % 3 == hc)
                        wait(act, down, e, HC * FT, user + 1 + FREE_DOWN)
                        act.activation(hhi[0:n, hc % 3, :], hf[0:n, hc % 2, :], ACT.Copy).then_inc(h_hi, 1)
                        if hc == PREPARE and (t < FT - 1 or not last):
                            prepare(*(e, t + 1) if t < FT - 1 else (e.plus(1), 0))
                        if fetch and hc >= 3:
                            next_weights(e, hc - 3)
                    wait(act, down, e, HC * FT, HC * (t + 1) + FREE_DOWN)
                    wait(act, gate_done, e, FT, t + 1)
                    wait(act, rows_free, e, FT, t + 1)
                    for j in range(FJ):
                        act.activation(ysb[:, t % 2, j, :], yb[j // 2][:, (j % 2) * D:(j % 2 + 1) * D], ACT.Copy,
                                       scale=gslot[:, t % 2, j:j + 1]).then_inc(y_read, 1)
                    if fetch:
                        for hc in range(HC - 3, HC):
                            next_weights(e, hc)

            experts(act, expert)

        @block.vector
        def _(dve):
            dve.sem_inc(w_split, HC)
            dve.sem_inc(mul_done, FREE_MUL)
            dve.wait_ge(consts_loaded, 32)
            dve.wait_ge(consts_made, 1)
            in_stats1 = Chain(dve, stats_chain1, 4)
            in_fac1 = Chain(dve, fac_chain1, 8)
            in_stats2 = Chain(dve, stats_chain2, 4)
            in_choose = Chain(dve, choose_chain, 14)
            in_place = Chain(dve, place_chain, 9)
            in_gate = Chain(dve, gate_chain, FT + 1)

            def statistics1(g, h):
                wait(dve, x_loaded[h], g, 16, 16)
                stand_apart(dve)
                in_stats1.begin(g, 2 * h)
                for j in range(HT):
                    last = dve.bn_stats(st1[:, h, j, :], xslot(g, h, j))
                in_stats1.link(last)
                stand_apart(dve)
                for j in range(HT):
                    last = dve.bn_aggr(mv1[:, h, j, :], st1[:, h, j, :])
                in_stats1.link(last)
                dve.tensor_scalar(ve1[:, h, 0, :], mv1[:, h, :, 1], LN_EPS, None, ALU.add)
                dve.tensor_scalar(ve1[:, h, 1, :], mv1[:, h, :, 1], float(D), None, ALU.mult).then_inc(stats1, 1)

            def factors1(g, h):
                wait(dve, pow1, g, 2, h + 1)
                in_fac1.begin(g, 4 * h)
                in_fac1.link(dve.tensor_tensor(nrm[:, :], pw1[:, h, 0, :], pw1[:, h, 1, :], ALU.mult))
                in_fac1.link(dve.tensor_scalar(rec[:, :], nrm[:, :], NORM_MIN, None, ALU.max))
                in_fac1.link(dve.reciprocal(rec[:, :], rec[:, :]))
                in_fac1.link(dve.scalar_tensor_tensor(out=sc1[:, h, :], in0=pw1[:, h, 0, :], scalar=float(D) ** 0.5,
                                                      in1=rec[:, :], op0=ALU.mult, op1=ALU.mult))
                dve.scalar_tensor_tensor(out=nb1[:, h, :], in0=mv1[:, h, :, 0], scalar=-1.0, in1=sc1[:, h, :],
                                         op0=ALU.mult, op1=ALU.mult).then_inc(fac1, 1)

            def split1(g, h):
                for k in range(KD):
                    wait(dve, split_hi, g, 4, 2 * h + k + 1)
                    dve.scalar_tensor_tensor(out=xTlo[:, h, k, :], in0=tA[k][:, :], scalar=gamma[:, k:k + 1],
                                             in1=xThi[:, h, k, :].bitcast(F32), op0=ALU.mult,
                                             op1=ALU.subtract).then_inc(split_lo, 1)

            def recurrence(g, h, ch):
                n = 2 * h + ch + 1
                wait(dve, sig_done, g, 4, n)
                wait(dve, kv_done, g, 4, n)
                dve.tensor_tensor_scan(y[:, h, ch, :], sig[:, ch, :], pkv[:, :],
                                       0.0 if h == 0 else y[:, 0, ch, T - 1:T], ALU.mult, ALU.add).then_inc(scan_done, 1)
                wait(dve, scan_done, g, 4, n)
                wait(dve, q_done, g, 4, n)
                wait(dve, back, g, 2, h - 1)
                dve.tensor_tensor(z[:, h, ch, :], pq[:, :], y[:, h, ch, :], ALU.mult).then_inc(z_done, 1)

            def residual(g, h):
                wait(dve, back, g, 2, h + 1)
                for m in range(HT // 2):
                    at = xslot(g, h, 2 * m, 2)
                    last = dve.tensor_tensor(at, at, tC[m][:, :], ALU.add)
                last.then_inc(x1_done, 1)
                wait(dve, x1_done, g, 2, h + 1)
                stand_apart(dve)
                in_stats2.begin(g, 2 * h)
                for j in range(HT):
                    last = dve.bn_stats(st2[:, h, j, :], xslot(g, h, j))
                in_stats2.link(last)
                stand_apart(dve)
                for j in range(HT):
                    last = dve.bn_aggr(mv2[:, h, j, :], st2[:, h, j, :])
                in_stats2.link(last)
                dve.tensor_scalar(ve2[:, h, :], mv2[:, h, :, 1], LN_EPS, None, ALU.add).then_inc(stats2, 1)

            def factors2(g, h):
                wait(dve, pow2, g, 2, h + 1)
                dve.scalar_tensor_tensor(out=nb2[:, h, :], in0=mv2[:, h, :, 0], scalar=-1.0, in1=sc2[:, h, :],
                                         op0=ALU.mult, op1=ALU.mult).then_inc(fac2, 1)

            def over_experts(ap):
                return ap.unsqueeze(2).to_broadcast([P, TILES, E])

            lg3 = lg.rearrange("p (t e) -> p t e", e=E)
            cum4 = cum.rearrange("p (k t e) -> p k t e", k=2, e=E)
            ranks = rank[:, :].unsqueeze(1).to_broadcast([P, TILES, E])

            def choose(g):
                wait(dve, logits, g, 2, 2)
                in_choose.begin(g)
                link = in_choose.link
                link(dve.reduce_max(mx[:, :], lg3, AXX))
                dve.tensor_tensor(dl[:, :, :], lg3, over_experts(mx[:, :]), ALU.subtract).then_inc(shifted, 1)
                wait(dve, exps, g, 1, 1)
                link(dve.reduce_sum(sm[:, :], ex[:, :, :], AXX))
                link(dve.reciprocal(rs[:, :], sm[:, :]))
                link(dve.tensor_tensor(raw[:, :, :], ex[:, :, :], over_experts(rs[:, :]), ALU.mult))
                for k in range(2):
                    p = raw if k == 0 else ex
                    link(dve.reduce_max(gate[:, k, :], p[:, :, :], AXX))
                    link(dve.tensor_tensor(eq[:, :, :], p[:, :, :], over_experts(gate[:, k, :]), ALU.is_equal))
                    link(dve.tensor_tensor(dl[:, :, :], eq[:, :, :], ranks, ALU.mult))
                    link(dve.reduce_max(top[:, k, :], dl[:, :, :], AXX))
                    ins = dve.tensor_tensor(mask[:, k, :, :], dl[:, :, :], over_experts(top[:, k, :]), ALU.is_equal)
                    if k == 0:
                        link(ins)
                        link(dve.scalar_tensor_tensor(
                            out=ex[:, :, :].rearrange("p t e -> p (t e)"),
                            in0=mask[:, 0, :, :].rearrange("p t e -> p (t e)"), scalar=0.0,
                            in1=raw[:, :, :].rearrange("p t e -> p (t e)"), op0=ALU.is_equal, op1=ALU.mult))
                    else:
                        ins.then_inc(masks, 1)
                in_choose.end()

            def place(g):
                wait(dve, counted, g, 1, 1)
                in_place.begin(g)
                link = in_place.link
                link(dve.tensor_scalar(cnt1[:, :], tot, float(CAP), None, ALU.min))
                dve.tensor_tensor(pos[:, 0, :, :], cum4[:, 0], mask[:, 0, :, :], ALU.mult)
                link(dve.tensor_tensor(pos[:, 1, :, :], cum4[:, 1],
                                       cnt1[:, :].unsqueeze(1).to_broadcast([P, TILES, E]), ALU.add))
                link(dve.tensor_tensor(pos[:, 1, :, :], pos[:, 1, :, :], mask[:, 1, :, :], ALU.mult))
                link(dve.reduce_sum(psel[:, :, :].rearrange("p k t -> p (k t)"),
                                    pos[:, :, :, :].rearrange("p k t e -> p (k t) e"), AXX))
                flat = [a[:, :, :].rearrange("p k t -> p (k t)") for a in (psel, gate, keep, top, slotf, sloti)]
                psel2, gate2, keep2, top2, slotf2, sloti2 = flat
                dve.scalar_tensor_tensor(out=keep2, in0=psel2, scalar=float(CAP), in1=gate2,
                                         op0=ALU.is_lt, op1=ALU.mult)
                link(dve.scalar_tensor_tensor(out=slotf2, in0=top2, scalar=-float(ESLOTS), in1=psel2,
                                              op0=ALU.mult, op1=ALU.add))
                link(dve.scalar_tensor_tensor(out=slotf2, in0=slotf2, scalar=slotbase[:, :], in1=dump[:, :],
                                              op0=ALU.add, op1=ALU.subtract))
                link(dve.scalar_tensor_tensor(out=slotf2, in0=keep2, scalar=0.0, in1=slotf2,
                                              op0=ALU.not_equal, op1=ALU.mult))
                wait(dve, scatter_done, g, 1, FREE_SCATTER)
                dve.tensor_tensor(sloti2, slotf2, dump[:, :], ALU.add)
                dve.tensor_copy(rows[:, :, GT1:GT2 + 1], keep[:, :, :].rearrange("p k t -> p t k"))
                dve.tensor_scalar(rows[:, :, EX1], top[:, 0, :], -1.0, float(E), ALU.mult, ALU.add)
                dve.tensor_copy(rows[:, :, TOK].bitcast(I32), tokid[:, :]).then_inc(routed, 1)
                wait(dve, routed, g, 1, 1)
                link(dve.tensor_scalar(slotbase[:, :], slotbase[:, :], float(CAP), None, ALU.add))
                link(dve.tensor_scalar(tokid[:, :], tokid[:, :], float(S), None, ALU.add))
                in_place.end()

            for k in range(KD):
                for m, (a, b) in enumerate(((0, 512), (512, NCH * P))):
                    dve.wait_ge(wq_hi, 2 * k + m + 1)
                    dve.tensor_tensor(wTlo[:, k, a:b], bank[2 * k + m][:, 0:b - a],
                                      wThi[:, k, a:b].bitcast(F32), ALU.subtract).then_inc(wq_lo, 1)

            def step(i):
                A, B, C, Dg = live(i, 1), live(i, 0), live(i, -1), live(i, -2)
                if A:
                    statistics1(i.plus(1), 0)
                if B:
                    recurrence(i, 0, 0)
                if Dg:
                    place(i.plus(-2))
                if A:
                    factors1(i.plus(1), 0)
                if C:
                    residual(i.plus(-1), 0)
                if B:
                    recurrence(i, 0, 1)
                if C:
                    factors2(i.plus(-1), 0)
                    residual(i.plus(-1), 1)
                if A:
                    split1(i.plus(1), 0)
                    statistics1(i.plus(1), 1)
                if B:
                    recurrence(i, 1, 0)
                if C:
                    factors2(i.plus(-1), 1)
                if A:
                    factors1(i.plus(1), 1)
                if B:
                    recurrence(i, 1, 1)
                if A:
                    split1(i.plus(1), 1)
                if C:
                    choose(i.plus(-1))

            pipeline(dve, step)

            def prepare(e, t):
                p = t % 2
                wait(dve, rows_loaded[p], e, 16 * FT // 2, 16 * (t // 2 + 1))
                dve.scalar_tensor_tensor(out=gsel[:, 0, :], in0=rows2[:, p, :, EX1], scalar=expert_no[:, :],
                                         in1=rows2[:, p, :, GT1], op0=ALU.is_equal, op1=ALU.mult)
                in_gate.begin(e, t)
                in_gate.link(dve.scalar_tensor_tensor(out=gsel[:, 1, :], in0=rows2[:, p, :, EX1],
                                                      scalar=expert_no[:, :], in1=rows2[:, p, :, GT2],
                                                      op0=ALU.not_equal, op1=ALU.mult))
                dve.tensor_tensor(gslot[:, p, :], gsel[:, 0, :], gsel[:, 1, :], ALU.add).then_inc(gate_done, 1)
                for k in range(KD):
                    wait(dve, fx_hi, e, KD * FT, KD * t + k + 1)
                    dve.tensor_tensor(xTlo[:, p, k, :], tA[k][:, :], xThi[:, p, k, :].bitcast(F32),
                                      ALU.subtract).then_inc(fx_lo, 1)

            prepare(Turn(0), 0)

            def next_weights(e, hc):
                wait(dve, w_hi, e, HC, hc + 1)
                dve.tensor_tensor(wlo[:, hc, :], stage[:, hc % STAGES, :], whi[:, hc, :].bitcast(F32),
                                  ALU.subtract).then_inc(w_split, 1)

            def expert(e, last):
                for t in range(FT):
                    fetch = t == FT - 1 and not last
                    for hc in range(HC):
                        n = P if hc < HC - 1 else HLAST
                        c = HC * t + hc
                        wait(dve, gelu_done, e, HC * FT, c + 1)
                        wait(dve, up1, e, HC * FT, c + 1)
                        dve.tensor_tensor(hf[0:n, hc % 2, :], up[hc % 2][1][0:n, :], gel[0:n, hc % 2, :],
                                          ALU.mult).then_inc(mul_done, 1)
                        wait(dve, h_hi, e, HC * FT, c + 1)
                        dve.tensor_tensor(hlo[0:n, hc % 3, :], hf[0:n, hc % 2, :], hhi[0:n, hc % 3, :].bitcast(F32),
                                          ALU.subtract).then_inc(h_lo, 1)
                        if hc == PREPARE and t < FT - 1:
                            prepare(e, t + 1)
                        elif hc == PREPARE and not last:
                            in_gate.begin(e, FT)
                            in_gate.link(dve.tensor_scalar(expert_no[:, :], expert_no[:, :], 1.0, None, ALU.add))
                            prepare(e.plus(1), 0)
                        if fetch and hc >= 3:
                            next_weights(e, hc - 3)
                    if fetch:
                        for hc in range(HC - 3, HC):
                            next_weights(e, hc)

            experts(dve, expert)

        @block.tensor
        def _(pe):
            pe.sem_inc(down, FREE_DOWN)
            pe.wait_ge(consts_made, 1)
            pe.wait_ge(consts_loaded, 32)
            PARTS = ((0, 0), (0, 1), (1, 0))

            def projection(g, h, ch):
                n = 2 * h + ch
                if ch == 0:
                    wait(pe, split_lo, g, 4, 2 * h + 2)
                for dst, which, free, done in ((pa, 2, sig_done, a_done), (pkv, 1, z_done, kv_done),
                                               (pq, 0, None, q_done)):
                    if free is not None:
                        wait(pe, free, g, 4, n)
                    cols = slice((which * KD + ch) * P, (which * KD + ch + 1) * P)
                    for m, (wp, xp) in enumerate(PARTS):
                        for k in range(KD):
                            last = pe.matmul(dst[:, :], (wThi, wTlo)[wp][:, k, cols], (xThi, xTlo)[xp][:, h, k, :],
                                             start=m == 0 and k == 0, stop=m == 2 and k == KD - 1)
                    last.then_inc(done, 1)

            def transpose1(g, h):
                wait(pe, norm1, g, 2, h + 1)
                wait(pe, split_lo, g, 4, 2 * h)
                for j in range(HT):
                    for k in range(KD):
                        last = pe.transpose(tA[k][:, j * P:(j + 1) * P], xn[:, j, k * P:(k + 1) * P], ident[:, :])
                last.then_inc(t1, 1)

            def transpose_back(g, h):
                wait(pe, z_done, g, 4, 2 * h + 2)
                if h == 0:
                    wait(pe, x2nT_done, g, 4, 0)
                else:
                    wait(pe, x1_done, g, 2, 1)
                for j in range(HT):
                    for k in range(KD):
                        at = (j % 2) * D + k * P
                        last = pe.transpose(tC[j // 2][:, at:at + P], z[:, h, k, j * P:(j + 1) * P], ident[:, :])
                last.then_inc(back, 1)

            def transpose2(g, h):
                wait(pe, norm2, g, 2, h + 1)
                if h == 0:
                    wait(pe, x1_done, g, 2, 2)
                else:
                    wait(pe, x2nT_done, g, 4, 2)
                for j in range(HT):
                    for k in range(KD):
                        last = pe.transpose(tC[k][:, j * P:(j + 1) * P], x2n[:, h, j, k * P:(k + 1) * P], ident[:, :])
                last.then_inc(t2, 1)

            def route(g, h):
                wait(pe, x2nT_done, g, 4, 2 * h + 2)
                if h == 0:
                    wait(pe, shifted, g, 1, 0)
                for j in range(HT):
                    for k in range(KD):
                        at = (h * HT + j) * E
                        last = pe.matmul(lg[:, at:at + E], x2nT[:, k, j * P:(j + 1) * P], router[:, k, :],
                                         start=k == 0, stop=k == KD - 1)
                last.then_inc(logits, 1)

            def count(g):
                wait(pe, masks, g, 1, 1)
                cum4 = cum.rearrange("p (k t e) -> p k t e", k=2, e=E)
                for t in range(TILES):
                    pe.matmul(cum4[:, :, t, :], before[:, :], mask[:, :, t, :], start=True, stop=t == 0)
                    for u in range(t):
                        pe.matmul(cum4[:, :, t, :], ones[:, :], mask[:, :, u, :], start=False, stop=u == t - 1)
                for t in range(TILES):
                    last = pe.matmul(tot, ones[:, :], mask[:, 0, t, :], start=t == 0, stop=t == TILES - 1)
                last.then_inc(counted, 1)

            pe.wait_ge(wq_loaded, 16)
            for k in range(KD):
                for c in range(NCH):
                    last = pe.transpose(bank[2 * k + c // 4][:, (c % 4) * P:(c % 4 + 1) * P],
                                        wraw[:, c, k * P:(k + 1) * P], ident[:, :])
            last.then_inc(wq_t, 1)
            pe.wait_ge(wq_lo, 2 * KD)

            def step(i):
                A, B, C, Dg = live(i, 1), live(i, 0), live(i, -1), live(i, -2)
                if B:
                    projection(i, 0, 0)
                if Dg:
                    count(i.plus(-2))
                if C:
                    transpose_back(i.plus(-1), 0)
                if B:
                    projection(i, 0, 1)
                if C:
                    transpose_back(i.plus(-1), 1)
                if A:
                    transpose1(i.plus(1), 0)
                if B:
                    projection(i, 1, 0)
                if C:
                    transpose2(i.plus(-1), 0)
                if B:
                    projection(i, 1, 1)
                if A:
                    transpose1(i.plus(1), 1)
                if C:
                    route(i.plus(-1), 0)
                    transpose2(i.plus(-1), 1)
                    route(i.plus(-1), 1)

            pipeline(pe, step)

            def prepare(e, t):
                p = t % 2
                wait(pe, rows_loaded[p], e, 16 * FT // 2, 16 * (t // 2 + 1))
                for k in range(KD):
                    for j in range(FJ):
                        last = pe.transpose(tA[k][:, j * P:(j + 1) * P], rows2[:, p, j, k * P:(k + 1) * P], ident[:, :])
                    last.then_inc(ft, 1)

            prepare(Turn(0), 0)
            pe.wait_ge(w_split0, HC)
            pe.wait_ge(z_done, 4 * G)
            pe.wait_ge(x2nT_done, 4 * G)

            def up_chunk(e, t, hc):
                n = P if hc < HC - 1 else HLAST
                c = HC * t + hc
                if t == 0:
                    wait(pe, w_split, e, HC, hc + 1)
                if hc == 0:
                    wait(pe, fx_lo, e, KD * FT, KD * (t + 1))
                user = c - 2 if hc >= 2 else c - hc - HC + max(q for q in range(HC) if q % 2 == hc)
                wait(pe, mul_done, e, HC * FT, user + 1 + FREE_MUL)
                for w, done in ((0, up0), (1, up1)):
                    for m, (wp, xp) in enumerate(PARTS):
                        for k in range(KD):
                            at = (w * KD + k) * P
                            last = pe.matmul(up[hc % 2][w][0:n, :], (whi, wlo)[wp][:, hc, at:at + n],
                                             (xThi, xTlo)[xp][:, t % 2, k, :],
                                             start=m == 0 and k == 0, stop=m == 2 and k == KD - 1)
                    last.then_inc(done, 1)

            def down_chunk(e, t, hc):
                n = P if hc < HC - 1 else HLAST
                wait(pe, h_lo, e, HC * FT, HC * t + hc + 1)
                if hc == 0:
                    wait(pe, y_read, e, FT * FJ, FJ * t + FJ)
                    pe.wait_ge(routed, G)
                for j in range(FJ):
                    for m, (wp, xp) in enumerate(PARTS):
                        last = pe.matmul(yb[j // 2][:, (j % 2) * D:(j % 2 + 1) * D],
                                         (hhi, hlo)[xp][0:n, hc % 3, j * P:(j + 1) * P],
                                         (whi, wlo)[wp][0:n, hc, 2 * KD * P:WCOL],
                                         start=hc == 0 and m == 0 and j % 2 == 0,
                                         stop=hc == HC - 1 and m == 2, skip_group_check=True)
                last.then_inc(down, 1)

            def expert(e, last):
                for t in range(FT):
                    for hc in range(HC):
                        up_chunk(e, t, hc)
                        if hc == PREPARE and (t < FT - 1 or not last):
                            prepare(*(e, t + 1) if t < FT - 1 else (e.plus(1), 0))
                        if hc >= 2:
                            down_chunk(e, t, hc - 2)
                    for hc in range(HC - 2, HC):
                        down_chunk(e, t, hc)

            experts(pe, expert)
    return nc


_INS = ["L0_attn_x", "L0_attn_w_qkva", "L0_attn_gamma", "L0_ffn_router_w", "L0_ffn_w0_kernel", "L0_ffn_w1_kernel",
        "L0_ffn_wo_kernel"]


def kernel(**inputs):
    import numpy as _np
    import concourse.bacc as _bacc
    from concourse import mybir as _mybir
    from concourse.bass_utils import run_bass_kernel_spmd as _run

    nc = _bacc.Bacc("TRN2", target_bir_lowering=False, num_devices=1)
    arrays, args = {}, []
    for name in _INS:
        a = _np.ascontiguousarray(inputs[name])
        arrays[f"in_{name}"] = a
        args.append(nc.dram_tensor(f"in_{name}", a.shape, _mybir.dt.from_np(a.dtype), kind="ExternalInput").ap())
    out = nc.dram_tensor("out_0", arrays["in_L0_attn_x"].shape, F32, kind="ExternalOutput").ap()
    build(nc, *args, out)
    r = _run(nc, [arrays], core_ids=[0])
    return r.results[0]["out_0"]
```

```python
from contextlib import ExitStack

import numpy as np

import concourse.bass as bass
from concourse import mybir

F32 = mybir.dt.float32
F32R = mybir.dt.float32r
BF16 = mybir.dt.bfloat16
I32 = mybir.dt.int32
ALU = mybir.AluOpType
ACT = mybir.ActivationFunctionType
AXX = mybir.AxisListType.X
P = 128
PREPARE = 6
LN_EPS = 1e-5
NORM_MIN = 1e-12


FREE_SCATTER = 2
FREE_MUL = 2
FREE_DOWN = 3
FREE_ROWS = 2


class Turn:

    def __init__(self, value, least=None):
        self.value = value
        self.fixed = least is None
        self.least = value if least is None else least

    def plus(self, n):
        return Turn(self.value + n, None if self.fixed else self.least + n)

    @property
    def parity(self):
        return self.least % 2

    def count(self, per, more):
        return self.value * per + more


def wait(eng, sem, turn, per, more):
    least = turn.least * per + more
    if turn.fixed and least <= 0:
        return
    assert least > 0
    eng.wait_ge(sem, turn.count(per, more))


class Chain:

    def __init__(self, eng, sem, per):
        self.eng, self.sem, self.per = eng, sem, per

    def begin(self, turn, done=0):
        self.turn, self.n = turn, done

    def link(self, instruction):
        self.n += 1
        instruction.then_inc(self.sem, 1)
        wait(self.eng, self.sem, self.turn, self.per, self.n)

    def end(self):
        assert self.n == self.per, (self.n, self.per)


def build(nc, x_in, w_qkva, gamma_in, router_in, w0_in, w1_in, wo_in, out):
    G, S, D = x_in.shape
    E, _, H = w0_in.shape
    CAP = (2 * S // E + 3) // 4 * 4
    KD = D // P
    TILES = S // P
    HT = TILES // 2
    T = HT * P
    NCH = 3 * D // P
    HC = -(-H // P)
    HLAST = H - (HC - 1) * P
    ROW = D + 4
    GT1, GT2, EX1, TOK = D, D + 1, D + 2, D + 3
    ESLOTS = G * CAP
    NSLOT = E * ESLOTS
    FT = ESLOTS // T
    FJ = T // P
    BATCH = 2
    NTOK = G * S
    WCOL = 2 * KD * P + D
    STAGES = 4
    XSLOTS = 3
    XG = TILES * D
    assert (G, KD, TILES, FT, T, FJ) == (8, 2, 8, 4, 512, 4) and E * 16 <= P

    slots = nc.dram_tensor("slots", [NSLOT + 2 * S, ROW], F32, kind="Internal").ap()
    sums = nc.dram_tensor("sums", [NTOK + T, D], F32, kind="Internal").ap()

    with ExitStack() as ctx:
        def sb(name, shape, dt=F32):
            return ctx.enter_context(nc.sbuf_tensor(name, shape, dt))

        def sem(name):
            return ctx.enter_context(nc.semaphore(name))

        ROWS2 = 2 * FJ * ROW
        xring = sb("xring", [P, 2 * XG + ROWS2])
        assert ROWS2 >= XG
        rows = sb("rows", [P, 2, TILES, ROW])
        xn = sb("xn", [P, HT, D])
        xThi = sb("xThi", [P, 2, KD, T], F32R)
        xTlo = sb("xTlo", [P, 2, KD, T], F32R)
        wThi = sb("wThi", [P, KD, 3 * D], F32R)
        wTlo = sb("wTlo", [P, KD, 3 * D], F32R)
        sig = sb("sig", [P, KD, T])
        y = sb("y", [P, 2, KD, T])
        z = sb("z", [P, 2, KD, T])
        x2nT = sb("x2nT", [P, KD, T])
        fill = sb("fill", [P, FJ, ROW])
        whi = sb("whi", [P, HC, WCOL], F32R)
        wlo = sb("wlo", [P, HC, WCOL], F32R)
        stage = sb("stage", [P, STAGES, WCOL])
        hhi = sb("hhi", [P, 3, T], F32R)
        hlo = sb("hlo", [P, 3, T], F32R)
        ident = sb("ident", [P, P])
        before = sb("before", [P, P], BF16)
        ones = sb("ones", [P, P], BF16)
        router = sb("router", [P, KD, E])
        gamma = sb("gamma", [P, KD])
        halves = sb("halves", [P, 2, 2, HT])
        rank = sb("rank", [P, E])
        dump = sb("dump", [P, 2 * TILES])
        slotbase = sb("slotbase", [P, 1])
        tokid = sb("tokid", [P, TILES])
        expert_no = sb("expert_no", [P, 1])
        st1 = sb("st1", [P, 2, HT, 6])
        mv1 = sb("mv1", [P, 2, HT, 2])
        ve1 = sb("ve1", [P, 2, 2, HT])
        pw1 = sb("pw1", [P, 2, 2, HT])
        nrm = sb("nrm", [P, 2, HT])
        rec = sb("rec", [P, 2, HT])
        sc1 = sb("sc1", [P, 2, HT])
        nb1 = sb("nb1", [P, 2, HT])
        st2 = sb("st2", [P, 2, HT, 6])
        mv2 = sb("mv2", [P, 2, HT, 2])
        ve2 = sb("ve2", [P, 2, HT])
        sc2 = sb("sc2", [P, 2, HT])
        nb2 = sb("nb2", [P, 2, HT])
        mx = sb("mx", [P, TILES])
        dl = sb("dl", [P, TILES, E])
        ex = sb("ex", [P, TILES, E])
        sm = sb("sm", [P, TILES])
        rs = sb("rs", [P, TILES])
        raw = sb("raw", [P, TILES, E])
        eq = sb("eq", [P, TILES, E])
        gate = sb("gate", [P, 2, TILES])
        top = sb("top", [P, 2, TILES])
        mask = sb("mask", [P, 2, TILES, E], BF16)
        cnt1 = sb("cnt1", [P, E])
        pos = sb("pos", [P, 2, TILES, E])
        psel = sb("psel", [P, 2, TILES])
        keep = sb("keep", [P, 2, TILES])
        slotf = sb("slotf", [P, 2, TILES])
        sloti = sb("sloti", [P, 2, 2, TILES], I32)
        gsel = sb("gsel", [P, 2, FJ])
        gslot = sb("gslot", [P, 2, FJ])

        wraw = rows[:, 0].rearrange("p j c -> p (j c)")[:, 0:NCH * D].rearrange("p (c d) -> p c d", c=NCH)
        rows2 = xring[:, 2 * XG:2 * XG + ROWS2].rearrange("p (b j c) -> p b j c", b=2, j=FJ)
        ysb = xring[:, 0:2 * FJ * D].rearrange("p (b j c) -> p b j c", b=2, j=FJ)
        gel = sig
        hf = y[:, 0]

        bank = [ctx.enter_context(nc.psum_tensor(f"bank{i}", [P, 512], F32)) for i in range(8)]
        tA = bank[0:2]
        pa, pkv, pq = bank[2], bank[3], bank[4]
        tC = bank[5:7]
        lg = bank[7][:, 0:TILES * E]
        cum = bank[7][:, 128:128 + 2 * TILES * E]
        tot = bank[7][:, 384:384 + E]
        up = [bank[2:4], bank[5:7]]
        yb = [bank[4], bank[7]]

        x_loaded = [sem(f"x_loaded{h}") for h in range(2)]
        consts_loaded = sem("consts_loaded")
        wq_loaded = sem("wq_loaded")
        consts_made = sem("consts_made")
        fill_made = sem("fill_made")
        emptied = sem("emptied")
        prefilled = [sem(f"prefilled{i}") for i in range(2)]
        sums_tail = sem("sums_tail")
        wq_t = sem("wq_t")
        wq_hi = sem("wq_hi")
        wq_lo = sem("wq_lo")
        consts_raw = sem("consts_raw")
        stats_chain1 = sem("stats_chain1")
        fac_chain1 = sem("fac_chain1")
        stats_chain2 = sem("stats_chain2")
        choose_chain = sem("choose_chain")
        place_chain = sem("place_chain")
        gate_chain = sem("gate_chain")
        stats1 = sem("stats1")
        pow1 = sem("pow1")
        fac1 = sem("fac1")
        norm1 = sem("norm1")
        t1 = sem("t1")
        split_hi = sem("split_hi")
        split_lo = sem("split_lo")
        a_done = sem("a_done")
        kv_done = sem("kv_done")
        q_done = sem("q_done")
        sig_done = sem("sig_done")
        scan_done = sem("scan_done")
        z_done = sem("z_done")
        back = sem("back")
        x1_done = sem("x1_done")
        stats2 = sem("stats2")
        pow2 = sem("pow2")
        fac2 = sem("fac2")
        norm2 = sem("norm2")
        x1_stored = [sem(f"x1_stored{h}") for h in range(2)]
        t2 = sem("t2")
        x2nT_done = sem("x2nT_done")
        logits = sem("logits")
        shifted = sem("shifted")
        exps = sem("exps")
        masks = sem("masks")
        counted = sem("counted")
        routed = sem("routed")
        scattered = [sem(f"scattered{h}") for h in range(2)]
        scatter_done = [sem(f"scatter_done{h}") for h in range(2)]
        w_staged = [sem(f"w_staged{i}") for i in range(STAGES)]
        w_hi0 = sem("w_hi0")
        w_split0 = sem("w_split0")
        w_hi = sem("w_hi")
        w_split = sem("w_split")
        rows_loaded = [sem(f"rows_loaded{i}") for i in range(2)]
        ft = sem("ft")
        fx_hi = sem("fx_hi")
        fx_lo = sem("fx_lo")
        gate_done = sem("gate_done")
        up0 = sem("up0")
        up1 = sem("up1")
        gelu_done = sem("gelu_done")
        mul_done = sem("mul_done")
        h_hi = sem("h_hi")
        h_lo = sem("h_lo")
        down = sem("down")
        y_read = sem("y_read")
        added = sem("added")
        rows_free = sem("rows_free")
        apart = {eng: sem(f"apart{i}") for i, eng in enumerate((nc.sync, nc.vector, nc.gpsimd))}
        out_stored = sem("out_stored")

        block = ctx.enter_context(nc.Block())

        def stand_apart(eng):
            eng.sem_inc(apart[eng], 1)

        def xslot(g, h, j, n=1):
            at = (g.value % XSLOTS) * XG + (h * HT + j) * D
            return xring[:, bass.ds(at, n * D)]

        def pipeline(eng, stage_fn):
            for i in range(-2, 2):
                stage_fn(Turn(i))
            with eng.Fori(2, G - 2, 2) as i:
                stage_fn(Turn(i, 2))
                stage_fn(Turn(i + 1, 3))
            for i in range(G - 2, G + 2):
                stage_fn(Turn(i))

        def live(i, ahead):
            return True if not i.fixed else 0 <= i.value + ahead < G

        def experts(eng, fn):
            with eng.Fori(0, E - 1) as e:
                fn(Turn(e, 0), False)
            fn(Turn(E - 1), True)

        def weight_loads(sync, e, hc):
            n = P if hc < HC - 1 else HLAST
            c = slice(hc * P, hc * P + n)
            s = hc % STAGES
            ev = e.value
            for k, w in enumerate((w0_in, w1_in)):
                src = w[bass.ds(ev, 1), :, c].rearrange("o (k p) h -> p (o k) h", p=P)
                dst = stage[:, s, k * KD * P:(k + 1) * KD * P].rearrange("p (k h) -> p k h", k=KD)[:, :, 0:n]
                sync.dma_start(dst, src).then_inc(w_staged[s], 16)
            sync.dma_start(stage[0:n, s, 2 * KD * P:WCOL],
                           wo_in[bass.ds(ev, 1), c, :].rearrange("o h m -> h (o m)")).then_inc(w_staged[s], 16)

        per_stage = [len(range(s, HC, STAGES)) for s in range(STAGES)]

        first_chunks = {-1: range(0, 2), 0: range(2, 6), 1: range(6, HC)}

        def staged(eng, e, hc):
            s = hc % STAGES
            wait(eng, w_staged[s], e, 48 * per_stage[s], 48 * (hc // STAGES + 1))

        def chunk_before(hc):
            return hc - STAGES if hc >= STAGES else max(c for c in range(HC) if c % STAGES == hc) - HC

        @block.sync
        def _(sync):
            def wait_apart(signal, turn, per, more):
                wait(sync, signal, turn, per, more)
                if not turn.fixed:
                    stand_apart(sync)

            def ring_half(g, h):
                at = (g.value % XSLOTS) * XG + h * HT * D
                return xring[:, bass.ds(at, HT * D)].rearrange("p (j c) -> p j c", j=HT)

            def load_x(g, h):
                if not g.fixed or g.value >= XSLOTS:
                    wait_apart(x1_stored[h], g, 16, -16 * (XSLOTS - 1))
                    wait_apart(norm2, g, 2, -2 * XSLOTS + h + 1)
                wait_apart(x_loaded[h], g, 16, 0)
                sync.dma_start(
                    ring_half(g, h),
                    x_in[bass.ds(g.value, 1), h * T:(h + 1) * T, :].rearrange("o (j p) c -> p (o j) c", p=P),
                ).then_inc(x_loaded[h], 16)

            def store_x1(g, h):
                wait_apart(x1_done, g, 2, h + 1)
                wait_apart(x1_stored[h], g, 16, 0)
                sync.dma_start(
                    sums[0:NTOK, :].rearrange("(g t) c -> g t c", g=G)[bass.ds(g.value, 1), h * T:(h + 1) * T, :]
                    .rearrange("o (j p) c -> p (o j) c", p=P),
                    ring_half(g, h),
                ).then_inc(x1_stored[h], 16)

            def first_weights(a, b):
                for hc in range(a, b):
                    sync.wait_ge(w_split0, chunk_before(hc) + 1)
                    weight_loads(sync, Turn(0), hc)

            def empty_slots(t, batches):
                tile_slots = slots[0:NSLOT, :].rearrange("(e t p j) c -> e t p j c", e=E, t=FT, j=FJ)
                for q in batches:
                    wait_apart(prefilled[q % 2], t, 16 * E // 2, 16 * BATCH * (q // 2))
                    for e in range(q * BATCH, (q + 1) * BATCH):
                        sync.dma_start(tile_slots[e, bass.ds(t.value, 1)].rearrange("o p j c -> p (o j) c"),
                                       fill[:, :, :]).then_inc(prefilled[q % 2], 16)

            def slots_are_empty(t):
                for filled in prefilled:
                    wait_apart(filled, t, 16 * E // 2, 16 * E // 2)
                sync.sem_inc(emptied, 2)

            load_x(Turn(0), 0)
            load_x(Turn(0), 1)
            sync.dma_start(gamma[:, :], gamma_in.rearrange("(k p) -> p k", p=P),
                           allow_slow_non_contiguous=True).then_inc(consts_loaded, 16)
            sync.dma_start(router[:, :, :], router_in.rearrange("(k p) e -> p k e", p=P)).then_inc(consts_loaded, 16)
            sync.dma_start(wraw, w_qkva.rearrange("(c p) d -> p c d", p=P)).then_inc(wq_loaded, 16)
            load_x(Turn(1), 0)
            load_x(Turn(1), 1)
            for hc in range(STAGES):
                weight_loads(sync, Turn(0), hc)
            sync.wait_ge(fill_made, 1)
            sync.dma_start(sums[NTOK:NTOK + T, :].rearrange("(p j) c -> p j c", p=P),
                           fill[:, :, 0:D]).then_inc(sums_tail, 16)
            load_x(Turn(2), 0)
            load_x(Turn(2), 1)
            batches = range(E // BATCH)
            empty_slots(Turn(0), batches)
            first_weights(STAGES, STAGES + 2)
            empty_slots(Turn(1), batches[0:2])
            first_weights(STAGES + 2, 2 * STAGES)
            empty_slots(Turn(1), batches[2:4])

            def step(i):
                for h in range(2):
                    if not i.fixed or i.value < G + 1:
                        store_x1(i.plus(-1), h)
                    if not i.fixed or i.value + 2 < G:
                        load_x(i.plus(2), h)

            slots_are_empty(Turn(0))
            step(Turn(1))
            first_weights(2 * STAGES, HC)
            with sync.Fori(1, FT - 1) as m:
                step(Turn(m * 2, 2))
                slots_are_empty(Turn(m, 1))
                empty_slots(Turn(m + 1, 2), batches[0:2])
                step(Turn(m * 2 + 1, 3))
                empty_slots(Turn(m + 1, 2), batches[2:4])
            slots_are_empty(Turn(FT - 1))
            for i in range(G - 2, G + 1):
                step(Turn(i))

            def load_rows(e, t):
                wait_apart(rows_free, e, FT, t + 1)
                for h in range(2):
                    sync.wait_ge(scatter_done[h], 2 * (t + 1) + FREE_SCATTER)
                src = slots[0:NSLOT, :].rearrange("(e s) c -> e s c", e=E)[bass.ds(e.value, 1), t * T:(t + 1) * T, :]
                sync.dma_start(rows2[:, t % 2], src.rearrange("o (p j) c -> p (o j) c", p=P)).then_inc(
                    rows_loaded[t % 2], 16)

            last_there = G - 1 - (G - 1 - 2) % XSLOTS
            for h in range(2):
                sync.wait_ge(x1_stored[h], 16 * (last_there + 1))
            sync.wait_ge(norm2, 2 * (last_there + 1))
            load_rows(Turn(0), 0)
            sync.wait_ge(w_split0, HC)

            def expert(e, last):
                for t in range(FT):
                    if t < FT - 1:
                        load_rows(e, t + 1)
                    elif not last:
                        load_rows(e.plus(1), 0)
                        for hc in range(HC):
                            wait_apart(w_split, e, HC, HC + chunk_before(hc) + 1)
                            weight_loads(sync, e.plus(1), hc)
                    if last:
                        wait_apart(rows_free, e, FT, t + 1 + FREE_ROWS)
                        a, b = t * NTOK // FT, (t + 1) * NTOK // FT
                        sync.dma_start(out.rearrange("g s c -> (g s) c")[a:b, :].rearrange("(p j) c -> p (j c)", p=P),
                                       sums[a:b, :].rearrange("(p j) c -> p (j c)", p=P)).then_inc(out_stored, 16)

            experts(sync, expert)
            sync.wait_ge(out_stored, 16 * FT)

        @block.gpsimd
        def _(pool):
            for h in range(2):
                pool.sem_inc(scatter_done[h], FREE_SCATTER)
            pool.sem_inc(rows_free, FREE_ROWS)
            pool.memset(ident[:, :], 0.0).then_inc(consts_raw, 1)
            pool.memset(before[:, :], 1.0).then_inc(consts_raw, 1)
            pool.wait_ge(consts_raw, 2)
            pool.affine_select(out=ident[:, :], in_=ident[:, :], compare_op=ALU.not_equal, fill=1.0, base=0,
                               pattern=[[-1, P]], channel_multiplier=1)
            pool.affine_select(out=before[:, :], in_=before[:, :], compare_op=ALU.is_gt, fill=0.0, base=0,
                               pattern=[[1, P]], channel_multiplier=-1)
            pool.memset(halves[:, :, 0, :], -0.5)
            pool.memset(halves[:, :, 1, :], 0.5)
            pool.memset(ones[:, :], 1.0)
            pool.memset(fill[:, :, 0:TOK], 0.0)
            pool.iota(fill[:, :, TOK].bitcast(I32), pattern=[[1, FJ]], base=NTOK,
                      channel_multiplier=FJ).then_inc(fill_made, 1)
            pool.iota(rank[:, :], pattern=[[-1, E]], base=E, channel_multiplier=0,
                      allow_small_or_imprecise_dtypes=True)
            pool.iota(dump[:, :], pattern=[[P, 2 * TILES]], base=NSLOT, channel_multiplier=1,
                      allow_small_or_imprecise_dtypes=True)
            pool.iota(tokid[:, :], pattern=[[P, TILES]], base=0, channel_multiplier=1,
                      allow_small_or_imprecise_dtypes=True)
            pool.memset(slotbase[:, :], float(E * ESLOTS))
            pool.memset(expert_no[:, :], 0.0).then_inc(consts_made, 1)

            def first_weights(hc):
                pool.wait_ge(w_hi0, hc + 1)
                pool.tensor_tensor(wlo[:, hc, :], stage[:, hc % STAGES, :], whi[:, hc, :].bitcast(F32),
                                   ALU.subtract).then_inc(w_split0, 1)

            def powers1(g):
                wait(pool, stats1, g, 1, 1)
                flat = [a[:, :, :, :].rearrange("p h k j -> p (h k j)") for a in (pw1, ve1, halves)]
                pool.tensor_tensor(flat[0], flat[1], flat[2], ALU.pow).then_inc(pow1, 1)

            def powers2(g, h):
                wait(pool, stats2, g, 2, h + 1)
                pool.tensor_tensor(sc2[:, h, :], ve2[:, h, :], halves[:, 0, 0, :], ALU.pow).then_inc(pow2, 1)

            def scatter(g, a, b):
                if a == 0:
                    wait(pool, emptied, g, 1, 2 - g.parity)
                    wait(pool, norm2, g, 2, 2)
                    wait(pool, routed, g, 1, 1)
                    stand_apart(pool)
                for t in range(a, b):
                    for k in range(2):
                        pool.indirect_dma_start(slots[:, :],
                                                bass.IndirectOffsetOnAxis(sloti[:, g.parity, k, t:t + 1], 0),
                                                rows[:, g.parity, t, :], None).then_inc(scattered[t // HT], 16)

            def end_scatter(g, h):
                wait(pool, scattered[h], g, 16 * 2 * HT, 16 * 2 * HT)
                pool.sem_inc(scatter_done[h], 1)

            def step(i):
                S, B, Dg = (live(i, n) for n in (2, 0, -2))
                first = first_chunks.get(i.value, ()) if i.fixed else ()
                before_last = i.fixed and i.value == G - 1
                for hc in first[0:len(first) // 2]:
                    first_weights(hc)
                if Dg:
                    scatter(i.plus(-2), 0, HT)
                if S:
                    powers1(i.plus(2))
                if before_last:
                    powers2(i, 0)
                if Dg:
                    scatter(i.plus(-2), HT, HT + 1)
                if B and not before_last:
                    powers2(i, 0)
                if Dg:
                    end_scatter(i.plus(-2), 0)
                    scatter(i.plus(-2), HT + 1, TILES)
                if B:
                    powers2(i, 1)
                for hc in first[len(first) // 2:]:
                    first_weights(hc)
                if Dg:
                    end_scatter(i.plus(-2), 1)

            pipeline(pool, step)

            pool.wait_ge(sums_tail, 16)
            for h in range(2):
                pool.wait_ge(x1_stored[h], 16 * G)

            def expert(e, last):
                for t in range(FT):
                    wait(pool, y_read, e, FT * FJ, FJ * (t + 1) + FJ)
                    stand_apart(pool)
                    for j in range(FJ):
                        idx = rows2[:, t % 2, j, TOK:TOK + 1].bitcast(I32)
                        pool.indirect_dma_start(sums[:, :], bass.IndirectOffsetOnAxis(idx, 0),
                                                ysb[:, t % 2, j, :], None, compute_op=ALU.add).then_inc(added, 16)
                    wait(pool, added, e, 16 * FJ * FT, 16 * FJ * (t + 1))
                    pool.sem_inc(rows_free, 1)

            experts(pool, expert)

        @block.scalar
        def _(act):
            act.sem_inc(y_read, FJ)
            act.wait_ge(consts_loaded, 32)

            def sigmoid(g, h, ch):
                wait(act, a_done, g, 4, 2 * h + ch + 1)
                act.activation(sig[:, ch, :], pa[:, :], ACT.Sigmoid).then_inc(sig_done, 1)

            def normalise1(g, h):
                wait(act, fac1, g, 1, 1)
                wait(act, t1, g, 2, h)
                for j in range(HT):
                    last = act.activation(xn[:, j, :], xslot(g, h, j), ACT.Identity,
                                          bias=nb1[:, h, j:j + 1], scale=sc1[:, h, j:j + 1])
                last.then_inc(norm1, 1)

            def split1(g, h):
                wait(act, t1, g, 2, h + 1)
                for k in range(KD):
                    act.activation(xThi[:, h, k, :], tA[k][:, :], ACT.Copy, scale=gamma[:, k:k + 1]).then_inc(split_hi, 1)

            def normalise2(g, h):
                wait(act, fac2, g, 2, h + 1)
                wait(act, t2, g, 2, h - 1)
                wait(act, scatter_done[h], g, 1, FREE_SCATTER - 1)
                for j in range(HT):
                    last = act.activation(rows[:, g.parity, h * HT + j, 0:D], xslot(g, h, j), ACT.Identity,
                                          bias=nb2[:, h, j:j + 1], scale=sc2[:, h, j:j + 1])
                last.then_inc(norm2, 1)

            def read_t2(g, h):
                wait(act, t2, g, 2, h + 1)
                wait(act, logits, g, 2, h)
                for k in range(KD):
                    act.activation(x2nT[:, k, :], tC[k][:, :], ACT.Copy).then_inc(x2nT_done, 1)

            def exponent(g):
                wait(act, shifted, g, 1, 1)
                act.activation(ex[:, :, :], dl[:, :, :], ACT.Exp).then_inc(exps, 1)

            def projection_weights():
                act.wait_ge(wq_t, 1)
                for k in range(KD):
                    for a, b in ((0, 512), (512, NCH * P)):
                        act.activation(wThi[:, k, a:b], bank[2 + 2 * k + a // 512][:, 0:b - a],
                                       ACT.Copy).then_inc(wq_hi, 1)

            def first_weights(hc):
                staged(act, Turn(0), hc)
                act.activation(whi[:, hc, :], stage[:, hc % STAGES, :], ACT.Copy).then_inc(w_hi0, 1)

            def prepare(e, t):
                for k in range(KD):
                    wait(act, ft, e, KD * FT, KD * t + k + 1)
                    act.activation(xThi[:, t % 2, k, :], tA[k][:, :], ACT.Copy).then_inc(fx_hi, 1)

            def step(i):
                A, B, C, Dg = live(i, 1), live(i, 0), live(i, -1), live(i, -2)
                if i.fixed and i.value == G + 1:
                    prepare(Turn(0), 0)
                first = first_chunks.get(i.value, ()) if i.fixed else ()
                if Dg:
                    exponent(i.plus(-2))
                if B:
                    sigmoid(i, 0, 0)
                if B:
                    sigmoid(i, 0, 1)
                if C:
                    normalise2(i.plus(-1), 0)
                if A:
                    normalise1(i.plus(1), 0)
                if i.fixed and i.value == -1:
                    projection_weights()
                for hc in first[0:len(first) // 2]:
                    first_weights(hc)
                if C:
                    read_t2(i.plus(-1), 0)
                if B:
                    sigmoid(i, 1, 0)
                if A:
                    split1(i.plus(1), 0)
                if C:
                    normalise2(i.plus(-1), 1)
                if B:
                    sigmoid(i, 1, 1)
                if A:
                    normalise1(i.plus(1), 1)
                if C:
                    read_t2(i.plus(-1), 1)
                for hc in first[len(first) // 2:]:
                    first_weights(hc)
                if A:
                    split1(i.plus(1), 1)

            pipeline(act, step)

            for h in range(2):
                act.wait_ge(x1_stored[h], 16 * G)

            def next_weights(e, hc):
                staged(act, e.plus(1), hc)
                wait(act, down, e, HC * FT, HC * (FT - 1) + hc + 1 + FREE_DOWN)
                act.activation(whi[:, hc, :], stage[:, hc % STAGES, :], ACT.Copy).then_inc(w_hi, 1)

            def expert(e, last):
                for t in range(FT):
                    fetch = t == FT - 1 and not last
                    for hc in range(HC):
                        n = P if hc < HC - 1 else HLAST
                        c = HC * t + hc
                        wait(act, up0, e, HC * FT, c + 1)
                        act.activation(gel[0:n, hc % 2, :], up[hc % 2][0][0:n, :],
                                       ACT.Gelu_apprx_tanh).then_inc(gelu_done, 1)
                        wait(act, mul_done, e, HC * FT, c + 1 + FREE_MUL)
                        user = c - 3 if hc >= 3 else c - hc - HC + max(q for q in range(HC) if q % 3 == hc)
                        wait(act, down, e, HC * FT, user + 1 + FREE_DOWN)
                        act.activation(hhi[0:n, hc % 3, :], hf[0:n, hc % 2, :], ACT.Copy).then_inc(h_hi, 1)
                        if hc == PREPARE and (t < FT - 1 or not last):
                            prepare(*(e, t + 1) if t < FT - 1 else (e.plus(1), 0))
                        if fetch and hc >= 3:
                            next_weights(e, hc - 3)
                    if fetch:
                        for hc in range(HC - 3, HC):
                            next_weights(e, hc)
                    wait(act, down, e, HC * FT, HC * (t + 1) + FREE_DOWN)
                    wait(act, gate_done, e, FT, t + 1)
                    wait(act, rows_free, e, FT, t + 1)
                    for j in range(FJ):
                        act.activation(ysb[:, t % 2, j, :], yb[j // 2][:, (j % 2) * D:(j % 2 + 1) * D], ACT.Copy,
                                       scale=gslot[:, t % 2, j:j + 1]).then_inc(y_read, 1)

            experts(act, expert)

        @block.vector
        def _(dve):
            dve.sem_inc(w_split, HC)
            dve.sem_inc(mul_done, FREE_MUL)
            dve.wait_ge(consts_loaded, 32)
            dve.wait_ge(consts_made, 1)
            in_stats1 = Chain(dve, stats_chain1, 4)
            in_fac1 = Chain(dve, fac_chain1, 4)
            in_stats2 = Chain(dve, stats_chain2, 4)
            in_choose = Chain(dve, choose_chain, 14)
            in_place = Chain(dve, place_chain, 9)
            in_gate = Chain(dve, gate_chain, FT + 1)

            def statistics1(g, h):
                wait(dve, x_loaded[h], g, 16, 16)
                stand_apart(dve)
                in_stats1.begin(g, 2 * h)
                for j in range(HT):
                    last = dve.bn_stats(st1[:, h, j, :], xslot(g, h, j))
                in_stats1.link(last)
                stand_apart(dve)
                for j in range(HT):
                    last = dve.bn_aggr(mv1[:, h, j, :], st1[:, h, j, :])
                in_stats1.link(last)
                if h == 1:
                    dve.tensor_scalar(ve1[:, :, 0, :], mv1[:, :, :, 1], LN_EPS, None, ALU.add)
                    dve.tensor_scalar(ve1[:, :, 1, :], mv1[:, :, :, 1], float(D), None, ALU.mult).then_inc(stats1, 1)

            def factors1(g):
                wait(dve, pow1, g, 1, 1)
                in_fac1.begin(g)
                in_fac1.link(dve.tensor_tensor(nrm[:, :, :], pw1[:, :, 0, :], pw1[:, :, 1, :], ALU.mult))
                in_fac1.link(dve.tensor_scalar(rec[:, :, :], nrm[:, :, :], NORM_MIN, None, ALU.max))
                in_fac1.link(dve.reciprocal(rec[:, :, :], rec[:, :, :]))
                in_fac1.link(dve.scalar_tensor_tensor(out=sc1[:, :, :], in0=pw1[:, :, 0, :], scalar=float(D) ** 0.5,
                                                      in1=rec[:, :, :], op0=ALU.mult, op1=ALU.mult))
                dve.scalar_tensor_tensor(out=nb1[:, :, :], in0=mv1[:, :, :, 0], scalar=-1.0, in1=sc1[:, :, :],
                                         op0=ALU.mult, op1=ALU.mult).then_inc(fac1, 1)
                in_fac1.end()

            def split1(g, h):
                for k in range(KD):
                    wait(dve, split_hi, g, 4, 2 * h + k + 1)
                    dve.scalar_tensor_tensor(out=xTlo[:, h, k, :], in0=tA[k][:, :], scalar=gamma[:, k:k + 1],
                                             in1=xThi[:, h, k, :].bitcast(F32), op0=ALU.mult,
                                             op1=ALU.subtract).then_inc(split_lo, 1)

            def recurrence(g, h, ch):
                n = 2 * h + ch + 1
                wait(dve, sig_done, g, 4, n)
                wait(dve, kv_done, g, 4, n)
                dve.tensor_tensor_scan(y[:, h, ch, :], sig[:, ch, :], pkv[:, :],
                                       0.0 if h == 0 else y[:, 0, ch, T - 1:T], ALU.mult, ALU.add).then_inc(scan_done, 1)
                wait(dve, scan_done, g, 4, n)
                wait(dve, q_done, g, 4, n)
                wait(dve, back, g, 2, h - 1)
                dve.tensor_tensor(z[:, h, ch, :], pq[:, :], y[:, h, ch, :], ALU.mult).then_inc(z_done, 1)

            def residual(g, h):
                wait(dve, back, g, 2, h + 1)
                for m in range(HT // 2):
                    at = xslot(g, h, 2 * m, 2)
                    last = dve.tensor_tensor(at, at, tC[m][:, :], ALU.add)
                last.then_inc(x1_done, 1)

            def statistics2(g, h):
                wait(dve, x1_done, g, 2, h + 1)
                stand_apart(dve)
                in_stats2.begin(g, 2 * h)
                for j in range(HT):
                    last = dve.bn_stats(st2[:, h, j, :], xslot(g, h, j))
                in_stats2.link(last)
                stand_apart(dve)
                for j in range(HT):
                    last = dve.bn_aggr(mv2[:, h, j, :], st2[:, h, j, :])
                in_stats2.link(last)
                dve.tensor_scalar(ve2[:, h, :], mv2[:, h, :, 1], LN_EPS, None, ALU.add).then_inc(stats2, 1)

            def factors2(g, h):
                wait(dve, pow2, g, 2, h + 1)
                dve.scalar_tensor_tensor(out=nb2[:, h, :], in0=mv2[:, h, :, 0], scalar=-1.0, in1=sc2[:, h, :],
                                         op0=ALU.mult, op1=ALU.mult).then_inc(fac2, 1)

            def over_experts(ap):
                return ap.unsqueeze(2).to_broadcast([P, TILES, E])

            lg3 = lg.rearrange("p (t e) -> p t e", e=E)
            cum4 = cum.rearrange("p (k t e) -> p k t e", k=2, e=E)
            ranks = rank[:, :].unsqueeze(1).to_broadcast([P, TILES, E])

            def shift(g):
                wait(dve, logits, g, 2, 2)
                in_choose.begin(g)
                in_choose.link(dve.reduce_max(mx[:, :], lg3, AXX))
                dve.tensor_tensor(dl[:, :, :], lg3, over_experts(mx[:, :]), ALU.subtract).then_inc(shifted, 1)

            def softmax(g):
                wait(dve, exps, g, 1, 1)
                link = in_choose.link
                link(dve.reduce_sum(sm[:, :], ex[:, :, :], AXX))
                link(dve.reciprocal(rs[:, :], sm[:, :]))
                link(dve.tensor_tensor(raw[:, :, :], ex[:, :, :], over_experts(rs[:, :]), ALU.mult))

            def choose(g, k):
                link = in_choose.link
                p = raw if k == 0 else ex
                link(dve.reduce_max(gate[:, k, :], p[:, :, :], AXX))
                link(dve.tensor_tensor(eq[:, :, :], p[:, :, :], over_experts(gate[:, k, :]), ALU.is_equal))
                link(dve.tensor_tensor(dl[:, :, :], eq[:, :, :], ranks, ALU.mult))
                link(dve.reduce_max(top[:, k, :], dl[:, :, :], AXX))
                ins = dve.tensor_tensor(mask[:, k, :, :], dl[:, :, :], over_experts(top[:, k, :]), ALU.is_equal)
                if k == 0:
                    link(ins)
                    link(dve.scalar_tensor_tensor(
                        out=ex[:, :, :].rearrange("p t e -> p (t e)"),
                        in0=mask[:, 0, :, :].rearrange("p t e -> p (t e)"), scalar=0.0,
                        in1=raw[:, :, :].rearrange("p t e -> p (t e)"), op0=ALU.is_equal, op1=ALU.mult))
                else:
                    ins.then_inc(masks, 1)
                    in_choose.end()

            def place(g):
                wait(dve, counted, g, 1, 1)
                in_place.begin(g)
                link = in_place.link
                link(dve.tensor_scalar(cnt1[:, :], tot, float(CAP), None, ALU.min))
                dve.tensor_tensor(pos[:, 0, :, :], cum4[:, 0], mask[:, 0, :, :], ALU.mult)
                link(dve.tensor_tensor(pos[:, 1, :, :], cum4[:, 1],
                                       cnt1[:, :].unsqueeze(1).to_broadcast([P, TILES, E]), ALU.add))
                link(dve.tensor_tensor(pos[:, 1, :, :], pos[:, 1, :, :], mask[:, 1, :, :], ALU.mult))
                link(dve.reduce_sum(psel[:, :, :].rearrange("p k t -> p (k t)"),
                                    pos[:, :, :, :].rearrange("p k t e -> p (k t) e"), AXX))
                flat = [a[:, :, :].rearrange("p k t -> p (k t)")
                        for a in (psel, gate, keep, top, slotf, sloti[:, g.parity])]
                psel2, gate2, keep2, top2, slotf2, sloti2 = flat
                row = rows[:, g.parity]
                dve.scalar_tensor_tensor(out=keep2, in0=psel2, scalar=float(CAP), in1=gate2,
                                         op0=ALU.is_lt, op1=ALU.mult)
                link(dve.scalar_tensor_tensor(out=slotf2, in0=top2, scalar=-float(ESLOTS), in1=psel2,
                                              op0=ALU.mult, op1=ALU.add))
                link(dve.scalar_tensor_tensor(out=slotf2, in0=slotf2, scalar=slotbase[:, :], in1=dump[:, :],
                                              op0=ALU.add, op1=ALU.subtract))
                link(dve.scalar_tensor_tensor(out=slotf2, in0=keep2, scalar=0.0, in1=slotf2,
                                              op0=ALU.not_equal, op1=ALU.mult))
                for h in range(2):
                    wait(dve, scatter_done[h], g, 1, FREE_SCATTER - 1)
                dve.tensor_tensor(sloti2, slotf2, dump[:, :], ALU.add)
                dve.tensor_copy(row[:, :, GT1:GT2 + 1], keep[:, :, :].rearrange("p k t -> p t k"))
                dve.tensor_scalar(row[:, :, EX1], top[:, 0, :], -1.0, float(E), ALU.mult, ALU.add)
                dve.tensor_copy(row[:, :, TOK].bitcast(I32), tokid[:, :]).then_inc(routed, 1)
                wait(dve, routed, g, 1, 1)
                link(dve.tensor_scalar(slotbase[:, :], slotbase[:, :], float(CAP), None, ALU.add))
                link(dve.tensor_scalar(tokid[:, :], tokid[:, :], float(S), None, ALU.add))
                in_place.end()

            def projection_weights():
                for k in range(KD):
                    for m, (a, b) in enumerate(((0, 512), (512, NCH * P))):
                        dve.wait_ge(wq_hi, 2 * k + m + 1)
                        dve.tensor_tensor(wTlo[:, k, a:b], bank[2 + 2 * k + m][:, 0:b - a],
                                          wThi[:, k, a:b].bitcast(F32), ALU.subtract).then_inc(wq_lo, 1)

            def prepare(e, t):
                p = t % 2
                wait(dve, rows_loaded[p], e, 16 * FT // 2, 16 * (t // 2 + 1))
                dve.scalar_tensor_tensor(out=gsel[:, 0, :], in0=rows2[:, p, :, EX1], scalar=expert_no[:, :],
                                         in1=rows2[:, p, :, GT1], op0=ALU.is_equal, op1=ALU.mult)
                in_gate.begin(e, t)
                in_gate.link(dve.scalar_tensor_tensor(out=gsel[:, 1, :], in0=rows2[:, p, :, EX1],
                                                      scalar=expert_no[:, :], in1=rows2[:, p, :, GT2],
                                                      op0=ALU.not_equal, op1=ALU.mult))
                dve.tensor_tensor(gslot[:, p, :], gsel[:, 0, :], gsel[:, 1, :], ALU.add).then_inc(gate_done, 1)
                for k in range(KD):
                    wait(dve, fx_hi, e, KD * FT, KD * t + k + 1)
                    dve.tensor_tensor(xTlo[:, p, k, :], tA[k][:, :], xThi[:, p, k, :].bitcast(F32),
                                      ALU.subtract).then_inc(fx_lo, 1)

            def step(i):
                S, A, B, C, Dg = (live(i, n) for n in (2, 1, 0, -1, -2))
                if i.fixed and i.value == G + 1:
                    prepare(Turn(0), 0)
                if Dg:
                    shift(i.plus(-2))
                if C:
                    residual(i.plus(-1), 0)
                if B:
                    split1(i, 1)
                    recurrence(i, 0, 0)
                if C:
                    statistics2(i.plus(-1), 0)
                if Dg:
                    softmax(i.plus(-2))
                if A:
                    factors1(i.plus(1))
                if C:
                    factors2(i.plus(-1), 0)
                if B:
                    recurrence(i, 0, 1)
                if C:
                    residual(i.plus(-1), 1)
                if Dg:
                    choose(i.plus(-2), 0)
                    choose(i.plus(-2), 1)
                if C:
                    statistics2(i.plus(-1), 1)
                if B:
                    recurrence(i, 1, 0)
                if C:
                    factors2(i.plus(-1), 1)
                if A:
                    if i.fixed and i.value == -1:
                        projection_weights()
                    split1(i.plus(1), 0)
                if Dg:
                    place(i.plus(-2))
                if S:
                    statistics1(i.plus(2), 0)
                if B:
                    recurrence(i, 1, 1)
                if S:
                    statistics1(i.plus(2), 1)

            pipeline(dve, step)


            def next_weights(e, hc):
                wait(dve, w_hi, e, HC, hc + 1)
                dve.tensor_tensor(wlo[:, hc, :], stage[:, hc % STAGES, :], whi[:, hc, :].bitcast(F32),
                                  ALU.subtract).then_inc(w_split, 1)

            def expert(e, last):
                for t in range(FT):
                    fetch = t == FT - 1 and not last
                    for hc in range(HC):
                        n = P if hc < HC - 1 else HLAST
                        c = HC * t + hc
                        wait(dve, gelu_done, e, HC * FT, c + 1)
                        wait(dve, up1, e, HC * FT, c + 1)
                        dve.tensor_tensor(hf[0:n, hc % 2, :], up[hc % 2][1][0:n, :], gel[0:n, hc % 2, :],
                                          ALU.mult).then_inc(mul_done, 1)
                        wait(dve, h_hi, e, HC * FT, c + 1)
                        dve.tensor_tensor(hlo[0:n, hc % 3, :], hf[0:n, hc % 2, :], hhi[0:n, hc % 3, :].bitcast(F32),
                                          ALU.subtract).then_inc(h_lo, 1)
                        if hc == PREPARE and t < FT - 1:
                            prepare(e, t + 1)
                        elif hc == PREPARE and not last:
                            in_gate.begin(e, FT)
                            in_gate.link(dve.tensor_scalar(expert_no[:, :], expert_no[:, :], 1.0, None, ALU.add))
                            prepare(e.plus(1), 0)
                        if fetch and hc >= 3:
                            next_weights(e, hc - 3)
                    if fetch:
                        for hc in range(HC - 3, HC):
                            next_weights(e, hc)

            experts(dve, expert)

        @block.tensor
        def _(pe):
            pe.sem_inc(down, FREE_DOWN)
            pe.wait_ge(consts_made, 1)
            pe.wait_ge(consts_loaded, 32)
            PARTS = ((0, 0), (0, 1), (1, 0))

            def projection(g, h, ch):
                n = 2 * h + ch
                if ch == 0:
                    wait(pe, split_lo, g, 4, 2 * h + 2)
                for dst, which, free, done in ((pa, 2, sig_done, a_done), (pkv, 1, scan_done, kv_done),
                                               (pq, 0, z_done, q_done)):
                    wait(pe, free, g, 4, n)
                    cols = slice((which * KD + ch) * P, (which * KD + ch + 1) * P)
                    for m, (wp, xp) in enumerate(PARTS):
                        for k in range(KD):
                            last = pe.matmul(dst[:, :], (wThi, wTlo)[wp][:, k, cols], (xThi, xTlo)[xp][:, h, k, :],
                                             start=m == 0 and k == 0, stop=m == 2 and k == KD - 1)
                    last.then_inc(done, 1)

            def transpose1(g, h):
                wait(pe, norm1, g, 2, h + 1)
                wait(pe, split_lo, g, 4, 2 * h)
                for j in range(HT):
                    for k in range(KD):
                        last = pe.transpose(tA[k][:, j * P:(j + 1) * P], xn[:, j, k * P:(k + 1) * P], ident[:, :])
                last.then_inc(t1, 1)

            def transpose_back(g, h):
                wait(pe, z_done, g, 4, 2 * h + 2)
                if h == 0:
                    wait(pe, x2nT_done, g, 4, 0)
                else:
                    wait(pe, x1_done, g, 2, 1)
                for j in range(HT):
                    for k in range(KD):
                        at = (j % 2) * D + k * P
                        last = pe.transpose(tC[j // 2][:, at:at + P], z[:, h, k, j * P:(j + 1) * P], ident[:, :])
                last.then_inc(back, 1)

            def transpose2(g, h):
                wait(pe, norm2, g, 2, h + 1)
                if h == 0:
                    wait(pe, x1_done, g, 2, 2)
                else:
                    wait(pe, x2nT_done, g, 4, 2)
                for j in range(HT):
                    for k in range(KD):
                        last = pe.transpose(tC[k][:, j * P:(j + 1) * P], rows[:, g.parity, h * HT + j, k * P:(k + 1) * P], ident[:, :])
                last.then_inc(t2, 1)

            def route(g, h):
                wait(pe, x2nT_done, g, 4, 2 * h + 2)
                wait(pe, shifted if h == 0 else routed, g, 1, 0)
                for j in range(HT):
                    for k in range(KD):
                        at = (h * HT + j) * E
                        last = pe.matmul(lg[:, at:at + E], x2nT[:, k, j * P:(j + 1) * P], router[:, k, :],
                                         start=k == 0, stop=k == KD - 1)
                last.then_inc(logits, 1)

            def count(g):
                wait(pe, masks, g, 1, 1)
                cum4 = cum.rearrange("p (k t e) -> p k t e", k=2, e=E)
                for t in range(TILES):
                    pe.matmul(cum4[:, :, t, :], before[:, :], mask[:, :, t, :], start=True, stop=t == 0)
                    for u in range(t):
                        pe.matmul(cum4[:, :, t, :], ones[:, :], mask[:, :, u, :], start=False, stop=u == t - 1)
                for t in range(TILES):
                    last = pe.matmul(tot, ones[:, :], mask[:, 0, t, :], start=t == 0, stop=t == TILES - 1)
                last.then_inc(counted, 1)

            pe.wait_ge(wq_loaded, 16)
            for k in range(KD):
                for c in range(NCH):
                    last = pe.transpose(bank[2 + 2 * k + c // 4][:, (c % 4) * P:(c % 4 + 1) * P],
                                        wraw[:, c, k * P:(k + 1) * P], ident[:, :])
            last.then_inc(wq_t, 1)

            def prepare(e, t):
                p = t % 2
                wait(pe, rows_loaded[p], e, 16 * FT // 2, 16 * (t // 2 + 1))
                for k in range(KD):
                    for j in range(FJ):
                        last = pe.transpose(tA[k][:, j * P:(j + 1) * P], rows2[:, p, j, k * P:(k + 1) * P], ident[:, :])
                    last.then_inc(ft, 1)

            def step(i):
                A, B, C, Dg = live(i, 1), live(i, 0), live(i, -1), live(i, -2)
                if i.fixed and i.value == 0:
                    pe.wait_ge(wq_lo, 2 * KD)
                if C:
                    transpose_back(i.plus(-1), 0)
                if B:
                    projection(i, 0, 0)
                if C:
                    transpose_back(i.plus(-1), 1)
                if B:
                    projection(i, 0, 1)
                if B:
                    projection(i, 1, 0)
                if C:
                    transpose2(i.plus(-1), 0)
                if A:
                    transpose1(i.plus(1), 0)
                if C:
                    route(i.plus(-1), 0)
                if Dg:
                    count(i.plus(-2))
                if B:
                    projection(i, 1, 1)
                if C:
                    transpose2(i.plus(-1), 1)
                if A:
                    transpose1(i.plus(1), 1)
                if i.fixed and i.value == G:
                    prepare(Turn(0), 0)
                if C:
                    route(i.plus(-1), 1)

            pipeline(pe, step)

            pe.wait_ge(w_split0, HC)
            pe.wait_ge(z_done, 4 * G)
            pe.wait_ge(x2nT_done, 4 * G)

            def up_chunk(e, t, hc):
                n = P if hc < HC - 1 else HLAST
                c = HC * t + hc
                if t == 0:
                    wait(pe, w_split, e, HC, hc + 1)
                if hc == 0:
                    wait(pe, fx_lo, e, KD * FT, KD * (t + 1))
                user = c - 2 if hc >= 2 else c - hc - HC + max(q for q in range(HC) if q % 2 == hc)
                wait(pe, mul_done, e, HC * FT, user + 1 + FREE_MUL)
                for w, done in ((0, up0), (1, up1)):
                    for m, (wp, xp) in enumerate(PARTS):
                        for k in range(KD):
                            at = (w * KD + k) * P
                            last = pe.matmul(up[hc % 2][w][0:n, :], (whi, wlo)[wp][:, hc, at:at + n],
                                             (xThi, xTlo)[xp][:, t % 2, k, :],
                                             start=m == 0 and k == 0, stop=m == 2 and k == KD - 1)
                    last.then_inc(done, 1)

            def down_chunk(e, t, hc):
                n = P if hc < HC - 1 else HLAST
                wait(pe, h_lo, e, HC * FT, HC * t + hc + 1)
                if hc == 0:
                    wait(pe, y_read, e, FT * FJ, FJ * t + FJ)
                    pe.wait_ge(routed, G)
                for j in range(FJ):
                    for m, (wp, xp) in enumerate(PARTS):
                        last = pe.matmul(yb[j // 2][:, (j % 2) * D:(j % 2 + 1) * D],
                                         (hhi, hlo)[xp][0:n, hc % 3, j * P:(j + 1) * P],
                                         (whi, wlo)[wp][0:n, hc, 2 * KD * P:WCOL],
                                         start=hc == 0 and m == 0 and j % 2 == 0,
                                         stop=hc == HC - 1 and m == 2, skip_group_check=True)
                last.then_inc(down, 1)

            def expert(e, last):
                for t in range(FT):
                    for hc in range(HC):
                        up_chunk(e, t, hc)
                        if hc == PREPARE and (t < FT - 1 or not last):
                            prepare(*(e, t + 1) if t < FT - 1 else (e.plus(1), 0))
                        if hc >= 2:
                            down_chunk(e, t, hc - 2)
                    for hc in range(HC - 2, HC):
                        down_chunk(e, t, hc)

            experts(pe, expert)
    return nc


_INS = ["L0_attn_x", "L0_attn_w_qkva", "L0_attn_gamma", "L0_ffn_router_w", "L0_ffn_w0_kernel", "L0_ffn_w1_kernel",
        "L0_ffn_wo_kernel"]


def kernel(**inputs):
    import numpy as _np
    import concourse.bacc as _bacc
    from concourse import mybir as _mybir
    from concourse.bass_utils import run_bass_kernel_spmd as _run

    nc = _bacc.Bacc("TRN2", target_bir_lowering=False, num_devices=1)
    arrays, args = {}, []
    for name in _INS:
        a = _np.ascontiguousarray(inputs[name])
        arrays[f"in_{name}"] = a
        args.append(nc.dram_tensor(f"in_{name}", a.shape, _mybir.dt.from_np(a.dtype), kind="ExternalInput").ap())
    out = nc.dram_tensor("out_0", arrays["in_L0_attn_x"].shape, F32, kind="ExternalOutput").ap()
    build(nc, *args, out)
    r = _run(nc, [arrays], core_ids=[0])
    return r.results[0]["out_0"]
```
